# Optimizing a Trainium2 kernel written in Bass

```python
import numpy as np
import jax
import jax.numpy as jnp

def _softmax(x, axis=-1):
    return jax.nn.softmax(x, axis=axis)

def _gelu(x):
    return jax.nn.gelu(x, approximate=True)

def _silu(x):
    return jax.nn.silu(x)

def _sigmoid(x):
    return jax.nn.sigmoid(x)

def _layernorm(x, axis=-1, eps=1e-05):
    m = jnp.mean(x, axis=axis, keepdims=True)
    v = jnp.var(x, axis=axis, keepdims=True)
    return (x - m) / jnp.sqrt(v + eps)

def _scatter_add(tgt, idx, src, axis=0):
    return tgt.at[idx].add(src)

def _segment_sum(src, seg, n):
    return jax.ops.segment_sum(src, seg, n)
kernel_name = 'mk_adj_resnorm_d2_adj_r2_602e7c'

def setup_inputs(seed: int=0):
    np.random.seed(seed)
    _w = jnp.asarray

    def _rec_inputs():
        import jax
        import jax.numpy as jnp
        _gk = jax.random.key(seed)
        x = -0.0002928 + 1 * jax.random.normal(jax.random.fold_in(_gk, 1), (8, 1024, 128), jnp.float32)
        _w = (1.0 + jnp.arange(1024, dtype=jnp.float32)) ** (-0.5)
        _w = _w / _w.mean()
        _pij = jnp.clip(0.0078125 * _w[:, None] * _w[None, :], 0.0, 1.0)
        _a = jax.random.uniform(jax.random.fold_in(_gk, 2), (8, 1024, 1024)) < _pij
        _a = jnp.logical_or(_a, jnp.swapaxes(_a, -1, -2))
        _a = jnp.logical_or(_a, jnp.eye(1024, dtype=bool))
        _af = _a.astype(jnp.float32)
        _af = _af * jax.random.uniform(jax.random.fold_in(_gk, 3), (8, 1024, 1024), jnp.float32, 0.05, 5.22011)
        adj = _af
        return (x, adj)
    x, adj = _rec_inputs()

    def _L0_gnn_setup():
        import jax, jax.numpy as jnp
        import numpy as np
        NEG_SLOPE = -0.2
        MASK_VAL = -9000000000000000.0
        key = jax.random.key(seed)
        k1, k2, k3, k4 = jax.random.split(key, 4)
        B, N, F, O = (8, 1024, 128, 128)
        x = jax.random.normal(k1, (B, N, F), dtype=jnp.float32)
        adj = jax.random.normal(k2, (B, N, N), dtype=jnp.float32)
        bw = 1.414 * np.sqrt(6.0 / (F + O))
        W_a = jax.random.uniform(k3, (F, O), minval=-bw, maxval=bw, dtype=jnp.float32)
        bb = 1.414 * np.sqrt(6.0 / (1 + O))
        bias = jax.random.uniform(k4, (1, O), minval=-bb, maxval=bb, dtype=jnp.float32)
        return {'x': x, 'adj': adj, 'W_a': W_a, 'bias': bias}
    _L0_gnn_all = _L0_gnn_setup()
    _L0_gnn_in = {k: v for k, v in _L0_gnn_all.items() if k in ('W_a', 'bias')}
    del _L0_gnn_all

    def _L1_gnn_setup():
        import jax, jax.numpy as jnp
        import numpy as np
        key = jax.random.key(seed)
        k1, k2, k3, k4 = jax.random.split(key, 4)
        B, N, F_in, F_out = (8, 1024, 128, 128)
        x = jax.random.normal(k1, (B, N, F_in), dtype=jnp.float32)
        adj = jax.random.uniform(k2, (B, N, N), dtype=jnp.float32)
        stdv = 1.0 / np.sqrt(F_out)
        weight = jax.random.uniform(k3, (F_in, F_out), dtype=jnp.float32, minval=-stdv, maxval=stdv)
        bias = jax.random.uniform(k4, (F_out,), dtype=jnp.float32, minval=-stdv, maxval=stdv)
        return {'x': x, 'adj': adj, 'weight': weight, 'bias': bias}
    _L1_gnn_all = _L1_gnn_setup()
    _L1_gnn_in = {k: v for k, v in _L1_gnn_all.items() if k in ('weight', 'bias')}
    del _L1_gnn_all
    return {'x': x, 'adj': adj, 'L0_gnn_W_a': _L0_gnn_in['W_a'], 'L0_gnn_bias': _L0_gnn_in['bias'], 'L1_gnn_weight': _L1_gnn_in['weight'], 'L1_gnn_bias': _L1_gnn_in['bias']}

def reference(x, adj, L0_gnn_W_a, L0_gnn_bias, L1_gnn_weight, L1_gnn_bias):
    import jax
    import jax.numpy as jnp

    def _L0_gnn_ref(x, adj, W_a, bias):
        import jax, jax.numpy as jnp
        import numpy as np
        NEG_SLOPE = -0.2
        MASK_VAL = -9000000000000000.0
        Xp = jnp.einsum('bnf,fo->bno', x, W_a)
        A = jnp.einsum('bno,bmo->bnm', Xp, Xp)
        mag = jnp.linalg.norm(A, axis=2, keepdims=True)
        A = A / (mag * jnp.swapaxes(mag, 1, 2))
        e = jnp.where(A >= 0, A, NEG_SLOPE * A)
        att = jnp.where(adj > 0, e, MASK_VAL)
        att = jax.nn.softmax(att, axis=2)
        h = jnp.einsum('bnm,bmf->bnf', att, x) + bias
        return jax.nn.elu(h)

    def _L1_gnn_ref(x, adj, weight, bias):
        import jax, jax.numpy as jnp
        import numpy as np
        support = jnp.einsum('bni,io->bno', x, weight)
        out = jnp.einsum('bnm,bmo->bno', adj, support)
        return out + bias
    x = _layernorm(x + _L0_gnn_ref(x, adj, L0_gnn_W_a, L0_gnn_bias), axis=-1)
    x = _layernorm(x + _L1_gnn_ref(x, adj, L1_gnn_weight, L1_gnn_bias), axis=-1)
    return x

_drawn_inputs = setup_inputs


def setup_inputs(seed=0):
    import zlib

    import numpy as np

    out = dict(_drawn_inputs(seed))
    spreads = {}
    factors = {'L0_gnn_W_a': 200.0, 'L1_gnn_bias': 7.665}
    for name, (base, spread) in spreads.items():
        noise = np.random.default_rng([zlib.crc32(name.encode()), seed]).standard_normal(out[name].shape)
        drawn = base * np.exp(spread * noise) if base else spread * noise
        out[name] = jnp.asarray(drawn.astype(out[name].dtype))
    for name, factor in factors.items():
        out[name] = (out[name] * factor).astype(out[name].dtype)
    return out
```

```python
from contextlib import ExitStack

import concourse.bass as bass
from concourse import mybir

F32 = mybir.dt.float32
F32R = mybir.dt.float32r
BF16 = mybir.dt.bfloat16
ALU = mybir.AluOpType
ACT = mybir.ActivationFunctionType

P = 128
SLOPE = -0.2
MASKED = -2.0 ** 126
TOP = 3.0e38
EPS = 1e-5
OLD, NEXT, OWN = "old", "next", "own"


class Step:

    def __init__(self, j, parity, old=True, next=True, own=True, x_loads=None):
        self.j, self.parity, self.old, self.next, self.own, self.x_loads = j, parity, old, next, own, x_loads


class Ring:

    def __init__(self, plan):
        self.plan = plan
        self.first = [item for part, item in plan if part == NEXT]
        self.old = sum(part == OLD for part, _ in plan)

    def begin(self, step):
        if not step.old:
            return len(self.first)
        lacking = self.old if step.own else self.old + len(self.first)
        return step.j * len(self.plan) + (len(self.first) - lacking)

    def number(self, step, item):
        if step is None:
            return self.first.index(item)
        has = {OWN: step.own, OLD: step.old, NEXT: step.next}
        return self.begin(step) + [it for part, it in self.plan if has[part]].index(item)

    def bank(self, step, item):
        if step is None:
            return self.number(None, item) % 2
        return self.number(Step(step.parity, step.parity, step.old, step.next, step.own), item) % 2


def gnn_kernel(nc, x, adj, w_a, bias0, weight, bias1, out):
    B, N, F = x.shape
    T = N // P
    HT = T // 2
    HN = N // 2
    CH = 2
    NCH = T // CH

    plan_a = []
    plan_d = []
    for i in range(T):
        plan_a += [(OWN, ("adjT", i, g)) for g in range(2)]
        plan_d += [(OLD, ("pT", T - 1, g)) for g in range(2)] if i == 0 else [(OWN, ("pT", i - 1, g)) for g in range(2)]
        if i == 1:
            plan_d += [(OLD, ("h", g)) for g in range(2)]
        if i == 3:
            plan_a += [(NEXT, ("xT", g)) for g in range(2)]
        if i == 4:
            plan_a += [(NEXT, ("xp", g)) for g in range(2)]
        if i == 5:
            plan_a += [(NEXT, ("gram", 0))] + [(NEXT, ("xpT", g)) for g in range(2)]
        if i == 6:
            plan_d += [(NEXT, ("y", g)) for g in range(2)] + [(OLD, ("w", 0))]
        if i == 7:
            plan_d += [(NEXT, ("xsT", g)) for g in range(2)] + [(OLD, ("w", 1))]
    ring_a, ring_d = Ring(plan_a), Ring(plan_d)

    with ExitStack() as ctx:
        def sb(name, shape, dt=F32):
            return ctx.enter_context(nc.sbuf_tensor(name, shape, dt))

        def psum(name, shape, dt=F32):
            return ctx.enter_context(nc.psum_tensor(name, shape, dt))

        def sem(name):
            return ctx.enter_context(nc.semaphore(name))

        adj_nat = sb("adj_nat", [P, NCH, CH, N])
        adj_t = sb("adj_t", [P, 2, T, N])
        p_t = sb("p_t", [P, 2, T, HN])
        score = sb("score", [P, 2, N])
        maskadd = sb("maskadd", [P, 2, N], BF16)
        x_nat = sb("x_nat", [P, 2, T, F])
        xp_t = sb("xp_t", [P, T, P])
        xp = sb("xp", [P, T, F])
        gram = sb("gram", [P, F])
        xs_hi = sb("xs_hi", [P, 2, N], F32R)
        xs_lo = sb("xs_lo", [P, 2, N], F32R)
        h_t = sb("h_t", [P, N])
        h = sb("h", [P, T, F])
        exp_h = sb("exp_h", [P, T, F])
        u_t = exp_h[:].rearrange("p t f -> p (t f)")
        y = sb("y", [P, T, F])
        x1 = sb("x1", [P, T, F])
        x1b = sb("x1b", [P, T, F])
        z = sb("z", [P, T, F])
        stats = sb("stats", [P, T, 6])
        mv = sb("mv", [P, T, 2])
        mv2 = sb("mv2", [P, T, 2])
        var_eps = sb("var_eps", [P, T])
        rstd = sb("rstd", [P, T])
        rstd2 = sb("rstd2", [P, T])
        magsq = sb("magsq", [P, T])
        rmag = sb("rmag", [P, T])
        neg_max = sb("neg_max", [P, 2, T])
        total = sb("total", [P, 2, T])
        rtotal = sb("rtotal", [P, T])
        neg_half = sb("neg_half", [P, T])
        ident = sb("ident", [P, P])
        wa_sb = sb("wa_sb", [F, F])
        w1_sb = sb("w1_sb", [F, F])
        b0_sb = sb("b0_sb", [P, F])
        b1_sb = sb("b1_sb", [P, F])

        s_ps = psum("s_ps", [P, 2, 512])
        bank_a = psum("bank_a", [P, 2, 512])
        bank_d = psum("bank_d", [P, 2, 512])
        h_ps = psum("h_ps", [P, 512])
        u_ps = psum("u_ps", [P, 512])

        const_in = sem("const_in")
        adj_in = [sem(f"adj_in{c}") for c in range(NCH)]
        x_in = [sem(f"x_in{c}") for c in range(2)]
        out_done = [sem(f"out_done{c}") for c in range(2)]
        setup = sem("setup")
        a_full, a_taken = sem("a_full"), sem("a_taken")
        d_full, d_taken = sem("d_full"), sem("d_taken")
        d_hi = sem("d_hi")
        score_full = sem("score_full")
        relu_ready = sem("relu_ready")
        mask_ready = sem("mask_ready")
        lrelu_ready = sem("lrelu_ready")
        negv_ready = sem("negv_ready")
        p_ready = sem("p_ready")
        h_full, ht_ready = sem("h_full"), sem("ht_ready")
        u_full, ut_ready = sem("u_full"), sem("ut_ready")
        exph_ready = sem("exph_ready")
        x_used = sem("x_used")
        stat1_ready, rstd1_ready = sem("stat1_ready"), sem("rstd1_ready")
        x1_ready, x1b_ready = sem("x1_ready"), sem("x1b_ready")
        stat2_ready, rstd2_ready = sem("stat2_ready"), sem("rstd2_ready")
        out_ready = sem("out_ready")
        rmag_ready, xs_ready = sem("rmag_ready"), sem("xs_ready")
        dve_chain, pool_chain = sem("dve_chain"), sem("pool_chain")

        def steps(eng, one_step):
            one_step(Step(0, 0, old=False, x_loads=1))
            with eng.Fori(0, (B - 2) // 2) as k:
                for u in range(2):
                    one_step(Step(k * 2 + (1 + u), (1 + u) % 2, x_loads=k + 2))
            one_step(Step(B - 1, (B - 1) % 2, next=False))
            one_step(Step(B, B % 2, next=False, own=False))

        met = {"sp": sem("met_sp"), "pool": sem("met_pool"), "dve": sem("met_dve")}

        def hold(eng, name):
            eng.sem_inc(met[name], 1)

        block = ctx.enter_context(nc.Block())

        @block.sync
        def _(sp):
            def load_adj(c, j):
                sp.dma_start(adj_nat[:, c], adj[j, c * CH * P:(c + 1) * CH * P, :].rearrange("(t p) m -> p t m", p=P)
                             ).then_inc(adj_in[c], 16)

            def load_x(j, parity):
                sp.dma_start(x_nat[:, parity], x[j].rearrange("(t p) f -> p t f", p=P)).then_inc(x_in[parity], 16)

            load_x(0, 0)
            sp.dma_start(wa_sb[:], w_a).then_inc(const_in, 16)
            load_adj(0, 0)
            load_x(1, 1)
            sp.dma_start(w1_sb[:], weight).then_inc(const_in, 16)
            sp.dma_start(b0_sb[:], bias0.broadcast_to([P, F])).then_inc(const_in, 16)
            sp.dma_start(b1_sb[:], bias1.rearrange("(a f) -> a f", a=1).broadcast_to([P, F])).then_inc(const_in, 16)
            for c in range(1, NCH):
                load_adj(c, 0)

            def one_step(st):
                if st.old and st.next:
                    sp.wait_ge(x_used, st.j)
                    hold(sp, "sp")
                    load_x(st.j + 1, 1 - st.parity)
                for c in range(NCH):
                    if st.next:
                        sp.wait_ge(a_full, ring_a.number(st, ("adjT", CH * c + CH - 1, 1)) + 1)
                        hold(sp, "sp")
                        sp.wait_ge(mask_ready, st.j * T + CH * (c + 1))
                        hold(sp, "sp")
                        load_adj(c, st.j + 1)
                if st.old:
                    for half in range(2):
                        sp.wait_ge(out_ready, (st.j - 1) * 2 + half + 1)
                        hold(sp, "sp")
                        sp.dma_start(out[st.j - 1, half * HN:(half + 1) * HN, :].rearrange("(t p) f -> p t f", p=P),
                                     z[:, half * HT:(half + 1) * HT]).then_inc(out_done[half], 16)

            steps(sp, one_step)
            for half in range(2):
                sp.wait_ge(out_done[half], 16 * (B + 1))

        @block.tensor
        def _(pe):
            def open_a(step, item):
                n = ring_a.number(step, item)
                if step is not None or n >= 2:
                    pe.wait_ge(a_taken, n - 1)
                return bank_a[:, ring_a.bank(step, item)]

            def open_d(step, item):
                n = ring_d.number(step, item)
                if step is not None or n >= 2:
                    pe.wait_ge(d_taken, n - 1)
                return bank_d[:, ring_d.bank(step, item)]

            def prep_xT(step, parity):
                for g in range(2):
                    dst = open_a(step, ("xT", g))
                    for t in range(HT):
                        mm = pe.transpose(dst[:, t * P:(t + 1) * P], x_nat[:, parity, g * HT + t, :], ident[:])
                    mm.then_inc(a_full, 1)

            def prep_xp(step):
                for g in range(2):
                    dst = open_a(step, ("xp", g))
                    pe.wait_ge(a_taken, ring_a.number(step, ("xT", g)) + 1)
                    for t in range(HT):
                        mm = pe.matmul(dst[:, t * F:(t + 1) * F], xp_t[:, g * HT + t, :], wa_sb[:], start=True, stop=True)
                    mm.then_inc(a_full, 1)

            def prep_gram(step):
                dst = open_a(step, ("gram", 0))
                pe.wait_ge(a_taken, ring_a.number(step, ("xp", 1)) + 1)
                for t in range(T):
                    mm = pe.matmul(dst[:, 0:F], xp[:, t, :], xp[:, t, :], start=(t == 0), stop=(t == T - 1))
                mm.then_inc(a_full, 1)

            def prep_xpT(step):
                for g in range(2):
                    dst = open_a(step, ("xpT", g))
                    for t in range(HT):
                        mm = pe.transpose(dst[:, t * P:(t + 1) * P], xp[:, g * HT + t, :], ident[:])
                    mm.then_inc(a_full, 1)

            def prep_y(step):
                for g in range(2):
                    dst = open_d(step, ("y", g))
                    pe.wait_ge(a_taken, ring_a.number(step, ("xpT", g)) + 1)
                    for t in range(HT):
                        mm = pe.matmul(dst[:, t * F:(t + 1) * F], xp_t[:, g * HT + t, :], gram[:], start=True, stop=True)
                    mm.then_inc(d_full, 1)

            def prep_xsT(step, j):
                pe.wait_ge(xs_ready, j + 1)
                for g in range(2):
                    dst = open_d(step, ("xsT", g))
                    for t in range(HT):
                        mm = pe.transpose(dst[:, t * P:(t + 1) * P], xp[:, g * HT + t, :], ident[:])
                    mm.then_inc(d_full, 1)

            def transpose_adj(st, i):
                for g in range(2):
                    dst = open_a(st, ("adjT", i, g))
                    for m in range(HT):
                        col = (g * HT + m) * P
                        mm = pe.transpose(dst[:, m * P:(m + 1) * P], adj_nat[:, i // CH, i % CH, col:col + P], ident[:])
                    mm.then_inc(a_full, 1)

            def scores(st, i, j):
                if i == 0:
                    pe.wait_ge(d_taken, ring_d.begin(st))
                if st.old or i > 0:
                    pe.wait_ge(negv_ready, j * T + i)
                rows = slice(i * P, (i + 1) * P)
                for hf in range(2):
                    cols = slice(hf * HN, (hf + 1) * HN)
                    hi, lo = xs_hi[:, st.parity], xs_lo[:, st.parity]
                    pe.matmul(s_ps[:, hf], hi[:, rows], hi[:, cols], start=True, stop=False)
                    pe.matmul(s_ps[:, hf], hi[:, rows], lo[:, cols], start=False, stop=False)
                    pe.matmul(s_ps[:, hf], lo[:, rows], hi[:, cols], start=False, stop=True).then_inc(score_full, 1)

            def transpose_p(st, i, j):
                pe.wait_ge(p_ready, j * T + i + 1)
                for g in range(2):
                    dst = open_d(st, ("pT", i, g))
                    for m in range(HT):
                        col = (g * HT + m) * P
                        mm = pe.transpose(dst[:, m * P:(m + 1) * P], score[:, i % 2, col:col + P], ident[:])
                    mm.then_inc(d_full, 1)

            def attend(st, half, j, parity, any_before):
                pe.wait_ge(d_taken, ring_d.number(st, ("pT", half * HT + HT - 1, 1)) + 1)
                if any_before:
                    pe.wait_ge(ht_ready, j * 2 + half)
                for m in range(T):
                    mm = pe.matmul(h_ps[:], x_nat[:, parity, m, :], p_t[:, half, m, :], start=(m == 0), stop=(m == T - 1))
                mm.then_inc(h_full, 1)

            def transpose_h(st, j):
                pe.wait_ge(ht_ready, j * 2 + 2)
                for g in range(2):
                    dst = open_d(st, ("h", g))
                    for t in range(HT):
                        mm = pe.transpose(dst[:, t * P:(t + 1) * P], h_t[:, (g * HT + t) * P:(g * HT + t + 1) * P], ident[:])
                    mm.then_inc(d_full, 1)

            def aggregate(j, parity, half, m0, m1):
                if m0 == 0:
                    pe.wait_ge(x1_ready, j + 1)
                if m0 == 0 and half == 1:
                    pe.wait_ge(ut_ready, j * 2 + 1)
                for m in range(m0, m1):
                    mm = pe.matmul(u_ps[:], x1[:, m, :], adj_t[:, parity, m, half * HN:(half + 1) * HN],
                                   start=(m == 0), stop=(m == T - 1))
                if m1 == T:
                    mm.then_inc(u_full, 1)

            def project(st, j, half):
                dst = open_d(st, ("w", half))
                pe.wait_ge(ut_ready, j * 2 + half + 1)
                for t in range(HT):
                    col = (half * HT + t) * P
                    mm = pe.matmul(dst[:, t * F:(t + 1) * F], u_t[:, col:col + P], w1_sb[:], start=True, stop=True)
                mm.then_inc(d_full, 1)

            pe.wait_ge(const_in, 64)
            pe.wait_ge(setup, 3)
            pe.wait_ge(x_in[0], 16)
            prep_xT(None, 0)
            prep_xp(None)
            prep_gram(None)
            prep_xpT(None)
            prep_y(None)
            prep_xsT(None, 0)

            def one_step(st):
                j = st.j
                for i in range(T):
                    if st.own:
                        if i % CH == 0:
                            pe.wait_ge(adj_in[i // CH], (j + 1) * 16)
                        transpose_adj(st, i)
                        scores(st, i, j)
                    if i > 0 and st.own:
                        transpose_p(st, i - 1, j)
                    if i == 0 and st.old:
                        transpose_p(st, T - 1, j - 1)
                        attend(st, 1, j - 1, 1 - st.parity, True)
                    if i == 1 and st.old:
                        transpose_h(st, j - 1)
                    if i == 3 and st.next:
                        pe.wait_ge(x_in[1 - st.parity], 16 * st.x_loads)
                        prep_xT(st, 1 - st.parity)
                    if i == 4:
                        if st.own:
                            attend(st, 0, j, st.parity, st.old)
                        if st.next:
                            prep_xp(st)
                    if i == 5:
                        if st.next:
                            prep_gram(st)
                            prep_xpT(st)
                        if st.old:
                            aggregate(j - 1, 1 - st.parity, 0, 0, T)
                    if i == 6:
                        if st.next:
                            prep_y(st)
                        if st.old:
                            project(st, j - 1, 0)
                            aggregate(j - 1, 1 - st.parity, 1, 0, HT)
                    if i == 7:
                        if st.old:
                            aggregate(j - 1, 1 - st.parity, 1, HT, T)
                        if st.next:
                            prep_xsT(st, j + 1)
                        if st.old:
                            project(st, j - 1, 1)

            steps(pe, one_step)

        @block.scalar
        def _(act):
            def take(step, item, dst):
                n = ring_a.number(step, item)
                act.wait_ge(a_full, n + 1)
                src = bank_a[:, ring_a.bank(step, item)]
                if item[0] == "gram":
                    src = src[:, 0:F]
                else:
                    src = src.rearrange("p (t f) -> p t f", t=HT)
                nc.scalar.copy(dst, src).then_inc(a_taken, 1)

            def prep_xT(step):
                for g in range(2):
                    take(step, ("xT", g), xp_t[:, g * HT:(g + 1) * HT, :])

            def prep_xp(step):
                for g in range(2):
                    take(step, ("xp", g), xp[:, g * HT:(g + 1) * HT, :])

            def prep_gram_xpT(step):
                take(step, ("gram", 0), gram[:])
                for g in range(2):
                    take(step, ("xpT", g), xp_t[:, g * HT:(g + 1) * HT, :])

            prep_xT(None)
            prep_xp(None)
            prep_gram_xpT(None)

            def one_step(st):
                j = st.j
                for i in range(T):
                    if st.own:
                        for g in range(2):
                            take(st, ("adjT", i, g), adj_t[:, st.parity, g * HT:(g + 1) * HT, i * P:(i + 1) * P])
                        for hf in range(2):
                            act.wait_ge(score_full, j * (2 * T) + (2 * i + hf + 1))
                            nc.scalar.activation(score[:, i % 2, hf * HN:(hf + 1) * HN], s_ps[:, hf], ACT.Relu,
                                                 scale=SLOPE - 1.0).then_inc(relu_ready, 1)
                    if i == 2 and st.old:
                        act.wait_ge(d_taken, ring_d.number(st, ("h", 1)) + 1)
                        nc.scalar.activation(exp_h[:], h[:], ACT.Exp).then_inc(exph_ready, 1)
                    if i == 3 and st.next:
                        prep_xT(st)
                    if i == 4 and st.next:
                        prep_xp(st)
                    if i == 5 and st.next:
                        prep_gram_xpT(st)
                    if st.own:
                        act.wait_ge(negv_ready, j * T + i + 1)
                        nc.scalar.activation(score[:, i % 2], score[:, i % 2], ACT.Exp, scale=-1.0,
                                             bias=neg_max[:, st.parity, i:i + 1],
                                             accum_out=total[:, st.parity, i:i + 1]).then_inc(p_ready, 1)

            steps(act, one_step)

        @block.gpsimd
        def _(pool):
            nc.gpsimd.memset(neg_half[:], -0.5).then_inc(setup, 1)
            nc.gpsimd.memset(ident[:], 0.0).then_inc(setup, 1)
            pool.wait_ge(setup, 2)
            nc.gpsimd.affine_select(out=ident[:], in_=ident[:], compare_op=ALU.not_equal, fill=1.0, base=0,
                                    pattern=[[-1, P]], channel_multiplier=1).then_inc(setup, 1)
            pool.wait_ge(const_in, 64)

            def inverse_norm(step):
                pool.wait_ge(d_taken, ring_d.number(step, ("y", 1)) + 1)
                nc.gpsimd.tensor_tensor(rmag[:], magsq[:], neg_half[:], ALU.pow).then_inc(rmag_ready, 1)

            def inverse_std(dst, src, count, sem_out):
                nc.gpsimd.tensor_scalar(var_eps[:, 0:src.shape[1]], src, EPS, 1.0, ALU.add, ALU.mult
                                        ).then_inc(pool_chain, 1)
                pool.wait_ge(pool_chain, count + 1)
                nc.gpsimd.tensor_tensor(dst, var_eps[:, 0:src.shape[1]], neg_half[:, 0:src.shape[1]], ALU.pow
                                        ).then_inc(sem_out, 1)

            inverse_norm(None)

            def one_step(st):
                j = st.j
                for i in range(T):
                    if st.own:
                        pool.wait_ge(mask_ready, j * T + i + 1)
                        for hf in range(2):
                            pool.wait_ge(relu_ready, j * (2 * T) + (2 * i + hf + 1))
                            cols = slice(hf * HN, (hf + 1) * HN)
                            nc.gpsimd.tensor_tensor(score[:, i % 2, cols], score[:, i % 2, cols],
                                                    maskadd[:, i % 2, cols], ALU.add).then_inc(lrelu_ready, 1)
                    if i == 3 and st.old:
                        pool.wait_ge(stat1_ready, j)
                        hold(pool, "pool")
                        inverse_std(rstd[:], mv[:, :, 1], (j - 1) * 3, rstd1_ready)
                    if i == 4 and st.old:
                        pool.wait_ge(x1_ready, j)
                        nc.gpsimd.tensor_tensor(x1b[:], x1[:], b1_sb[:].unsqueeze(1).broadcast_to([P, T, F]), ALU.add
                                                ).then_inc(x1b_ready, 1)
                    if i == 6:
                        if st.next:
                            inverse_norm(st)
                        if st.old:
                            pool.wait_ge(stat2_ready, (j - 1) * 2 + 1)
                            hold(pool, "pool")
                            inverse_std(rstd2[:, 0:HT], mv2[:, 0:HT, 1], (j - 1) * 3 + 1, rstd2_ready)
                    if i == 7 and st.old:
                        pool.wait_ge(stat2_ready, (j - 1) * 2 + 2)
                        hold(pool, "pool")
                        inverse_std(rstd2[:, HT:T], mv2[:, HT:T, 1], (j - 1) * 3 + 2, rstd2_ready)

            steps(pool, one_step)

        @block.vector
        def _(dve):
            LINKS = 5

            def link(ins, n):
                ins.then_inc(dve_chain, 1)
                dve.wait_ge(dve_chain, n)

            def full(step, item):
                dve.wait_ge(d_full, ring_d.number(step, item) + 1)
                return bank_d[:, ring_d.bank(step, item)]

            def row_mask(j, i):
                if i % CH == 0:
                    dve.wait_ge(adj_in[i // CH], (j + 1) * 16)
                nc.vector.tensor_scalar(maskadd[:, i % 2], adj_nat[:, i // CH, i % CH], 0.0, MASKED,
                                        ALU.is_le, ALU.mult).then_inc(mask_ready, 1)

            def negate_and_max(st, i):
                dve.wait_ge(lrelu_ready, st.j * (2 * T) + (2 * i + 2))
                hold(dve, "dve")
                nc.vector.tensor_tensor_reduce(score[:, i % 2], s_ps[:].rearrange("p a n -> p (a n)"), score[:, i % 2],
                                               -1.0, TOP, ALU.add, ALU.min,
                                               neg_max[:, st.parity, i:i + 1]).then_inc(negv_ready, 1)

            def take_p(st, i, j, any_before):
                if i % HT == 0 and any_before:
                    dve.wait_ge(h_full, j * 2 + (i // HT - 1))
                for g in range(2):
                    src = full(st, ("pT", i, g))
                    nc.vector.tensor_copy(p_t[:, i // HT, g * HT:(g + 1) * HT, (i % HT) * P:(i % HT + 1) * P],
                                          src.rearrange("p (m n) -> p m n", m=HT)).then_inc(d_taken, 1)

            def take_h(j, half):
                dve.wait_ge(h_full, j * 2 + half + 1)
                nc.vector.tensor_copy(h_t[:, half * HN:(half + 1) * HN], h_ps[:]).then_inc(ht_ready, 1)

            def take_u(j, half):
                dve.wait_ge(u_full, j * 2 + half + 1)
                nc.vector.tensor_copy(u_t[:, half * HN:(half + 1) * HN], u_ps[:]).then_inc(ut_ready, 1)

            def norm_squares(step):
                for g in range(2):
                    src = full(step, ("y", g))
                    dve.wait_ge(a_taken, ring_a.number(step, ("xp", g)) + 1)
                    for t in range(HT):
                        r = g * HT + t
                        last = nc.vector.tensor_tensor_reduce(y[:, r, :], src[:, t * F:(t + 1) * F], xp[:, r, :], 1.0, 0.0,
                                                              ALU.mult, ALU.add, magsq[:, r:r + 1])
                    last.then_inc(d_taken, 1)

            def scale_xp(step, j):
                dve.wait_ge(rmag_ready, j + 1)
                for r in range(T):
                    last = nc.vector.tensor_scalar(xp[:, r, :], xp[:, r, :], rmag[:, r:r + 1], None, ALU.mult)
                last.then_inc(xs_ready, 1)

            def split_xsT(step, j, parity):
                for g in range(2):
                    src = full(step, ("xsT", g))
                    cols = slice(g * HN, (g + 1) * HN)
                    nc.vector.tensor_copy(xs_hi[:, parity, cols], src).then_inc(d_hi, 1)
                    dve.wait_ge(d_hi, j * 2 + g + 1)
                    nc.vector.tensor_tensor(xs_lo[:, parity, cols], src, xs_hi[:, parity, cols].bitcast(F32),
                                            ALU.subtract).then_inc(d_taken, 1)

            def normalise(dst, src, mean_var, inv, tiles, done):
                for r in tiles:
                    last = nc.vector.tensor_scalar(dst[:, r, :], src[:, r, :], mean_var[:, r, 0:1], inv[:, r:r + 1],
                                                   ALU.subtract, ALU.mult)
                last.then_inc(done, 1)

            def statistics(src, mean_var, tiles, links, done):
                for r in tiles:
                    last = nc.vector.bn_stats(stats[:, r, :], src[:, r, :])
                last.then_inc(dve_chain, 1)
                dve.wait_ge(dve_chain, links)
                hold(dve, "dve")
                for r in tiles:
                    last = nc.vector.bn_aggr(mean_var[:, r, :], stats[:, r, :])
                last.then_inc(done, 1)

            def finish_layer0(st, j):
                dve.wait_ge(p_ready, j * T + T)
                link(nc.vector.reciprocal(rtotal[:], total[:, 1 - st.parity, :]), j * LINKS + 1)
                for g in range(2):
                    src = full(st, ("h", g))
                    for t in range(HT):
                        r = g * HT + t
                        last = nc.vector.scalar_tensor_tensor(h[:, r, :], src[:, t * F:(t + 1) * F], rtotal[:, r:r + 1],
                                                              b0_sb[:], ALU.mult, ALU.add)
                    last.then_inc(d_taken, 1)

            def add_residual0(st, j, parity):
                dve.wait_ge(d_taken, ring_d.number(st, ("h", 1)) + 1)
                nc.vector.scalar_tensor_tensor(y[:], h[:], 0.0, x_nat[:, parity], ALU.max, ALU.add).then_inc(x_used, 1)
                dve.wait_ge(x_used, j + 1)
                dve.wait_ge(exph_ready, j + 1)
                link(nc.vector.scalar_tensor_tensor(y[:], exp_h[:], 1.0, y[:], ALU.min, ALU.add), j * LINKS + 2)

            def finish_layer1(st, j, half):
                tiles = range(half * HT, (half + 1) * HT)
                src = full(st, ("w", half))
                if half == 0:
                    dve.wait_ge(x1b_ready, j + 1)
                dve.wait_ge(out_done[half], (j + 1) * 16)
                zh = z[:, half * HT:(half + 1) * HT, :]
                nc.vector.tensor_tensor(zh, src.rearrange("p (t f) -> p t f", t=HT), x1b[:, half * HT:(half + 1) * HT, :],
                                        ALU.add).then_inc(d_taken, 1)
                dve.wait_ge(d_taken, ring_d.number(st, ("w", half)) + 1)
                statistics(z, mv2, tiles, j * LINKS + 4 + half, stat2_ready)

            def store_norm(j, half):
                dve.wait_ge(rstd2_ready, j * 2 + half + 1)
                normalise(z, z, mv2, rstd2, range(half * HT, (half + 1) * HT), out_ready)

            for half in range(2):
                nc.vector.memset(z[:, half * HT, 0:1], 0.0).then_inc(out_done[half], 16)
            dve.wait_ge(const_in, 64)
            norm_squares(None)
            row_mask(0, 0)
            scale_xp(None, 0)
            split_xsT(None, 0, 0)

            def one_step(st):
                j = st.j
                for i in range(T):
                    if st.own:
                        if i + 1 < T:
                            row_mask(j, i + 1)
                        elif st.next:
                            row_mask(j + 1, 0)
                        if i > 0:
                            take_p(st, i - 1, j, st.old)
                    if i == 0 and st.old:
                        take_p(st, T - 1, j - 1, True)
                    if st.own:
                        negate_and_max(st, i)
                    if i == 0 and st.old:
                        take_h(j - 1, 1)
                    if i == 1 and st.old:
                        finish_layer0(st, j - 1)
                    if i == 2 and st.old:
                        add_residual0(st, j - 1, 1 - st.parity)
                        statistics(y, mv, range(T), (j - 1) * LINKS + 3, stat1_ready)
                    if i == 3 and st.old:
                        dve.wait_ge(rstd1_ready, j)
                        normalise(x1, y, mv, rstd, range(T), x1_ready)
                    if i == 4 and st.own:
                        take_h(j, 0)
                    if i == 5 and st.old:
                        take_u(j - 1, 0)
                    if i == 6:
                        if st.next:
                            norm_squares(st)
                        if st.old:
                            finish_layer1(st, j - 1, 0)
                    if i == 7:
                        if st.old:
                            store_norm(j - 1, 0)
                        if st.next:
                            scale_xp(st, j + 1)
                        if st.old:
                            take_u(j - 1, 1)
                        if st.next:
                            split_xsT(st, j + 1, 1 - st.parity)
                        if st.old:
                            finish_layer1(st, j - 1, 1)
                            store_norm(j - 1, 1)

            steps(dve, one_step)


_INS = ["x", "adj", "L0_gnn_W_a", "L0_gnn_bias", "L1_gnn_weight", "L1_gnn_bias"]
_OUTS = [((8, 1024, 128), "float32")]


def kernel(**inputs):
    import numpy as _np
    import concourse.bacc as _bacc
    from concourse import mybir as _mybir
    from concourse.bass_utils import run_bass_kernel_spmd as _run

    nc = _bacc.Bacc("TRN2", target_bir_lowering=False, num_devices=1)
    arrays, args = {}, []
    for name in _INS:
        a = _np.ascontiguousarray(inputs[name])
        arrays[f"in_{name}_dram"] = a
        args.append(nc.dram_tensor(f"in_{name}_dram", a.shape, _mybir.dt.from_np(a.dtype), kind="ExternalInput").ap())
    for i, (shape, dtype) in enumerate(_OUTS):
        dt = _mybir.dt.from_np(_np.dtype(dtype))
        args.append(nc.dram_tensor(f"out_{i}_dram", shape, dt, kind="ExternalOutput").ap())
    gnn_kernel(nc, *args)
    r = _run(nc, [arrays], core_ids=[0])
    return r.results[0]["out_0_dram"]
```

```python
from contextlib import ExitStack

import concourse.bass as bass
from concourse import mybir

F32 = mybir.dt.float32
F32R = mybir.dt.float32r
BF16 = mybir.dt.bfloat16
ALU = mybir.AluOpType
ACT = mybir.ActivationFunctionType

P = 128
SLOPE = -0.2
MASKED = -2.0 ** 126
TOP = 3.0e38
EPS = 1e-5
OLD, NEXT, OWN = "old", "next", "own"


class Step:

    def __init__(self, j, parity, old=True, next=True, own=True):
        self.j, self.parity, self.old, self.next, self.own = j, parity, old, next, own


class Ring:

    def __init__(self, plan):
        self.plan = plan
        self.first = [item for part, item in plan if part == NEXT]
        self.old = sum(part == OLD for part, _ in plan)

    def begin(self, step):
        if not step.old:
            return len(self.first)
        lacking = self.old if step.own else self.old + len(self.first)
        return step.j * len(self.plan) + (len(self.first) - lacking)

    def number(self, step, item):
        if step is None:
            return self.first.index(item)
        has = {OWN: step.own, OLD: step.old, NEXT: step.next}
        return self.begin(step) + [it for part, it in self.plan if has[part]].index(item)

    def bank(self, step, item):
        if step is None:
            return self.number(None, item) % 2
        return self.number(Step(step.parity, step.parity, step.old, step.next, step.own), item) % 2


def gnn_kernel(nc, x, adj, w_a, bias0, weight, bias1, out):
    B, N, F = x.shape
    T = N // P
    HT = T // 2
    HN = N // 2
    QT = T // 4
    QN = N // 4
    CH = 2
    NCH = T // CH

    plan_a = []
    plan_d = []
    for i in range(T):
        for plan, g in ((plan_a, 0), (plan_d, 1)):
            plan += [(OLD, ("pT", T - 1, g)) if i == 0 else (OWN, ("pT", i - 1, g))]
        plan_a += [(OWN, ("adjT", i, g)) for g in range(2)]
        if i == 0:
            plan_a += [(NEXT, ("xT", g)) for g in range(2)]
            plan_d += [(OLD, ("h", g)) for g in range(2)]
        if i == 1:
            plan_a += [(NEXT, ("xp", g)) for g in range(2)]
        if i == 2:
            plan_a += [(NEXT, ("gram", 0))]
        if i == 3:
            plan_a += [(NEXT, ("xpT", g)) for g in range(2)]
            plan_d += [(NEXT, ("y", g)) for g in range(2)]
        if i == 5:
            plan_d += [(NEXT, ("xsT", g)) for g in range(2)]
            plan_d += [(OLD, ("w", 0))]
        if i == 7:
            plan_d += [(OLD, ("w", 1))]
    ring_a, ring_d = Ring(plan_a), Ring(plan_d)

    with ExitStack() as ctx:
        def sb(name, shape, dt=F32):
            return ctx.enter_context(nc.sbuf_tensor(name, shape, dt))

        def psum(name, shape, dt=F32):
            return ctx.enter_context(nc.psum_tensor(name, shape, dt))

        def sem(name):
            return ctx.enter_context(nc.semaphore(name))

        adj_nat = sb("adj_nat", [P, NCH, CH, N])
        adj_t = sb("adj_t", [P, 2, T, N])
        p_t = sb("p_t", [P, 2, T, QN])
        score = sb("score", [P, 2, N])
        maskadd = sb("maskadd", [P, 2, N], BF16)
        x_next = sb("x_next", [P, T, F])
        x_nat = sb("x_nat", [P, 2, T, F])
        xp_t = sb("xp_t", [P, T, P])
        xp = sb("xp", [P, T, F])
        gram = sb("gram", [P, F])
        xs_hi = sb("xs_hi", [P, 2, N], F32R)
        xs_lo = sb("xs_lo", [P, 2, N], F32R)
        h_t = sb("h_t", [P, N])
        h = sb("h", [P, T, F])
        exp_h = sb("exp_h", [P, T, F])
        u_t = exp_h[:].rearrange("p t f -> p (t f)")
        y = sb("y", [P, T, F])
        x1 = sb("x1", [P, T, F])
        x1b = sb("x1b", [P, T, F])
        z = sb("z", [P, T, F])
        stats = sb("stats", [P, T, 6])
        mv = sb("mv", [P, T, 2])
        mv2 = sb("mv2", [P, T, 2])
        var_eps = sb("var_eps", [P, T])
        rstd = sb("rstd", [P, T])
        rstd2 = sb("rstd2", [P, T])
        magsq = sb("magsq", [P, T])
        rmag = sb("rmag", [P, T])
        neg_max = sb("neg_max", [P, 2, T])
        total = sb("total", [P, 2, T])
        rtotal = sb("rtotal", [P, T])
        neg_half = sb("neg_half", [P, T])
        ident = sb("ident", [P, P])
        wa_sb = sb("wa_sb", [F, F])
        w1_sb = sb("w1_sb", [F, F])
        b0_sb = sb("b0_sb", [P, F])
        b1_sb = sb("b1_sb", [P, F])

        s_ps = psum("s_ps", [P, 2, 512])
        bank_a = psum("bank_a", [P, 2, 512])
        bank_d = psum("bank_d", [P, 2, 512])
        h_ps = psum("h_ps", [P, 512])
        u_ps = psum("u_ps", [P, 512])

        const_in = sem("const_in")
        adj_in = [sem(f"adj_in{c}") for c in range(NCH)]
        x_in, x_copied = sem("x_in"), sem("x_copied")
        out_done = [sem(f"out_done{c}") for c in range(2)]
        setup = sem("setup")
        a_full, a_taken = sem("a_full"), sem("a_taken")
        d_full, d_taken = sem("d_full"), sem("d_taken")
        d_hi = sem("d_hi")
        score_full = sem("score_full")
        relu_ready = sem("relu_ready")
        mask_ready = sem("mask_ready")
        lrelu_ready = sem("lrelu_ready")
        negv_ready = sem("negv_ready")
        p_ready = sem("p_ready")
        h_full, ht_ready = sem("h_full"), sem("ht_ready")
        u_full, ut_ready = sem("u_full"), sem("ut_ready")
        exph_ready = sem("exph_ready")
        x_used = sem("x_used")
        stat1_ready, rstd1_ready = sem("stat1_ready"), sem("rstd1_ready")
        x1_ready, x1b_ready = sem("x1_ready"), sem("x1b_ready")
        stat2_ready, rstd2_ready = sem("stat2_ready"), sem("rstd2_ready")
        out_ready = sem("out_ready")
        rmag_ready, xs_ready = sem("rmag_ready"), sem("xs_ready")
        dve_chain, pool_chain = sem("dve_chain"), sem("pool_chain")

        def steps(eng, one_step):
            one_step(Step(0, 0, old=False))
            with eng.Fori(0, (B - 2) // 2) as k:
                for u in range(2):
                    one_step(Step(k * 2 + (1 + u), (1 + u) % 2))
            one_step(Step(B - 1, (B - 1) % 2, next=False))
            one_step(Step(B, B % 2, next=False, own=False))

        met = {"sp": sem("met_sp"), "pool": sem("met_pool"), "dve": sem("met_dve")}

        def hold(eng, name):
            eng.sem_inc(met[name], 1)

        block = ctx.enter_context(nc.Block())

        @block.sync
        def _(sp):
            def load_adj(c, j):
                sp.dma_start(adj_nat[:, c], adj[j, c * CH * P:(c + 1) * CH * P, :].rearrange("(t p) m -> p t m", p=P)
                             ).then_inc(adj_in[c], 16)

            def load_x(j):
                sp.dma_start(x_next[:], x[j].rearrange("(t p) f -> p t f", p=P)).then_inc(x_in, 16)

            load_x(0)
            sp.dma_start(wa_sb[:], w_a).then_inc(const_in, 16)
            sp.dma_start(w1_sb[:], weight).then_inc(const_in, 16)
            sp.dma_start(b0_sb[:], bias0.broadcast_to([P, F])).then_inc(const_in, 16)
            sp.dma_start(b1_sb[:], bias1.rearrange("(a f) -> a f", a=1).broadcast_to([P, F])).then_inc(const_in, 16)
            for c in range(NCH):
                load_adj(c, 0)

            def one_step(st):
                if st.next:
                    sp.wait_ge(a_full, ring_a.begin(st))
                    hold(sp, "sp")
                    sp.wait_ge(x_copied, st.j + 1)
                    hold(sp, "sp")
                    load_x(st.j + 1)
                for c in range(NCH):
                    if st.next:
                        sp.wait_ge(a_full, ring_a.number(st, ("adjT", CH * c + CH - 1, 1)) + 1)
                        hold(sp, "sp")
                        sp.wait_ge(mask_ready, st.j * T + CH * (c + 1))
                        hold(sp, "sp")
                        load_adj(c, st.j + 1)
                if st.old:
                    for half in range(2):
                        sp.wait_ge(out_ready, (st.j - 1) * 2 + half + 1)
                        hold(sp, "sp")
                        sp.dma_start(out[st.j - 1, half * HN:(half + 1) * HN, :].rearrange("(t p) f -> p t f", p=P),
                                     z[:, half * HT:(half + 1) * HT]).then_inc(out_done[half], 16)

            steps(sp, one_step)
            for half in range(2):
                sp.wait_ge(out_done[half], 16 * (B + 1))

        @block.tensor
        def _(pe):
            def open_a(step, item):
                n = ring_a.number(step, item)
                if step is not None or n >= 2:
                    pe.wait_ge(a_taken, n - 1)
                return bank_a[:, ring_a.bank(step, item)]

            def open_d(step, item):
                n = ring_d.number(step, item)
                if step is not None or n >= 2:
                    pe.wait_ge(d_taken, n - 1)
                return bank_d[:, ring_d.bank(step, item)]

            def prep_xT(step, j):
                pe.wait_ge(x_in, (j + 1) * 16)
                for g in range(2):
                    dst = open_a(step, ("xT", g))
                    for t in range(HT):
                        mm = pe.transpose(dst[:, t * P:(t + 1) * P], x_next[:, g * HT + t, :], ident[:])
                    mm.then_inc(a_full, 1)

            def prep_xp(step):
                for g in range(2):
                    dst = open_a(step, ("xp", g))
                    pe.wait_ge(a_taken, ring_a.number(step, ("xT", g)) + 1)
                    for t in range(HT):
                        mm = pe.matmul(dst[:, t * F:(t + 1) * F], xp_t[:, g * HT + t, :], wa_sb[:], start=True, stop=True)
                    mm.then_inc(a_full, 1)

            def prep_gram(step):
                dst = open_a(step, ("gram", 0))
                pe.wait_ge(a_taken, ring_a.number(step, ("xp", 1)) + 1)
                for t in range(T):
                    mm = pe.matmul(dst[:, 0:F], xp[:, t, :], xp[:, t, :], start=(t == 0), stop=(t == T - 1))
                mm.then_inc(a_full, 1)

            def prep_xpT(step):
                for g in range(2):
                    dst = open_a(step, ("xpT", g))
                    for t in range(HT):
                        mm = pe.transpose(dst[:, t * P:(t + 1) * P], xp[:, g * HT + t, :], ident[:])
                    mm.then_inc(a_full, 1)

            def prep_y(step):
                for g in range(2):
                    dst = open_d(step, ("y", g))
                    pe.wait_ge(a_taken, ring_a.number(step, ("xpT", g)) + 1)
                    for t in range(HT):
                        mm = pe.matmul(dst[:, t * F:(t + 1) * F], xp_t[:, g * HT + t, :], gram[:], start=True, stop=True)
                    mm.then_inc(d_full, 1)

            def prep_xsT(step, j):
                pe.wait_ge(xs_ready, j + 1)
                for g in range(2):
                    dst = open_d(step, ("xsT", g))
                    for t in range(HT):
                        mm = pe.transpose(dst[:, t * P:(t + 1) * P], xp[:, g * HT + t, :], ident[:])
                    mm.then_inc(d_full, 1)

            def transpose_adj(st, i):
                for g in range(2):
                    dst = open_a(st, ("adjT", i, g))
                    for m in range(HT):
                        col = (g * HT + m) * P
                        mm = pe.transpose(dst[:, m * P:(m + 1) * P], adj_nat[:, i // CH, i % CH, col:col + P], ident[:])
                    mm.then_inc(a_full, 1)

            def scores(st, i, j):
                if i == 0:
                    pe.wait_ge(d_taken, ring_d.begin(st) - (2 if st.old else 0))
                if st.old or i > 0:
                    pe.wait_ge(negv_ready, j * T + i)
                rows = slice(i * P, (i + 1) * P)
                for hf in range(2):
                    cols = slice(hf * HN, (hf + 1) * HN)
                    hi, lo = xs_hi[:, st.parity], xs_lo[:, st.parity]
                    pe.matmul(s_ps[:, hf], hi[:, rows], hi[:, cols], start=True, stop=False)
                    pe.matmul(s_ps[:, hf], hi[:, rows], lo[:, cols], start=False, stop=False)
                    pe.matmul(s_ps[:, hf], lo[:, rows], hi[:, cols], start=False, stop=True).then_inc(score_full, 1)

            def transpose_p(st, i, j):
                pe.wait_ge(p_ready, j * T + i + 1)
                for g, (opened, filled) in enumerate(((open_a, a_full), (open_d, d_full))):
                    dst = opened(st, ("pT", i, g))
                    for m in range(HT):
                        col = (g * HT + m) * P
                        mm = pe.transpose(dst[:, m * P:(m + 1) * P], score[:, i % 2, col:col + P], ident[:])
                    mm.then_inc(filled, 1)

            def attend(st, q, j, parity, any_before):
                pe.wait_ge(a_taken, ring_a.number(st, ("pT", q * QT + QT - 1, 0)) + 1)
                pe.wait_ge(d_taken, ring_d.number(st, ("pT", q * QT + QT - 1, 1)) + 1)
                if any_before:
                    pe.wait_ge(ht_ready, j * 4 + q)
                if q == 0:
                    pe.wait_ge(x_copied, j + 1)
                for m in range(T):
                    mm = pe.matmul(h_ps[:, 0:QN], x_nat[:, parity, m, :], p_t[:, q % 2, m, :],
                                   start=(m == 0), stop=(m == T - 1))
                mm.then_inc(h_full, 1)

            def transpose_h(st, j):
                pe.wait_ge(ht_ready, j * 4 + 4)
                for g in range(2):
                    dst = open_d(st, ("h", g))
                    for t in range(HT):
                        mm = pe.transpose(dst[:, t * P:(t + 1) * P], h_t[:, (g * HT + t) * P:(g * HT + t + 1) * P], ident[:])
                    mm.then_inc(d_full, 1)

            def aggregate(j, parity, half, m0, m1):
                if m0 == 0:
                    pe.wait_ge(x1_ready, j + 1)
                if m0 == 0 and half == 1:
                    pe.wait_ge(ut_ready, j * 2 + 1)
                for m in range(m0, m1):
                    mm = pe.matmul(u_ps[:], x1[:, m, :], adj_t[:, parity, m, half * HN:(half + 1) * HN],
                                   start=(m == 0), stop=(m == T - 1))
                if m1 == T:
                    mm.then_inc(u_full, 1)

            def project(st, j, half):
                dst = open_d(st, ("w", half))
                pe.wait_ge(ut_ready, j * 2 + half + 1)
                for t in range(HT):
                    col = (half * HT + t) * P
                    mm = pe.matmul(dst[:, t * F:(t + 1) * F], u_t[:, col:col + P], w1_sb[:], start=True, stop=True)
                mm.then_inc(d_full, 1)

            pe.wait_ge(const_in, 64)
            pe.wait_ge(setup, 3)
            prep_xT(None, 0)
            prep_xp(None)
            prep_gram(None)
            prep_xpT(None)
            prep_y(None)
            prep_xsT(None, 0)

            def one_step(st):
                j = st.j
                for i in range(T):
                    if st.own:
                        scores(st, i, j)
                        if i > 0:
                            transpose_p(st, i - 1, j)
                    if i == 0 and st.old:
                        transpose_p(st, T - 1, j - 1)
                    if st.own:
                        if i % CH == 0:
                            pe.wait_ge(adj_in[i // CH], (j + 1) * 16)
                        transpose_adj(st, i)
                    if i == 0:
                        if st.old:
                            attend(st, 3, j - 1, 1 - st.parity, True)
                        if st.next:
                            prep_xT(st, j + 1)
                        if st.old:
                            transpose_h(st, j - 1)
                    if i == 1 and st.next:
                        prep_xp(st)
                    if i == 2:
                        if st.next:
                            prep_gram(st)
                        if st.own:
                            attend(st, 0, j, st.parity, st.old)
                    if i == 3:
                        if st.next:
                            prep_xpT(st)
                            prep_y(st)
                        if st.old:
                            aggregate(j - 1, 1 - st.parity, 0, 0, HT)
                    if i == 4:
                        if st.old:
                            aggregate(j - 1, 1 - st.parity, 0, HT, T)
                        if st.own:
                            attend(st, 1, j, st.parity, True)
                    if i == 5:
                        if st.next:
                            prep_xsT(st, j + 1)
                        if st.old:
                            aggregate(j - 1, 1 - st.parity, 1, 0, HT)
                            project(st, j - 1, 0)
                    if i == 6 and st.old:
                        aggregate(j - 1, 1 - st.parity, 1, HT, T)
                    if i == 7:
                        if st.old:
                            project(st, j - 1, 1)
                        if st.own:
                            attend(st, 2, j, st.parity, True)

            steps(pe, one_step)

        @block.scalar
        def _(act):
            def take(step, item, dst):
                n = ring_a.number(step, item)
                act.wait_ge(a_full, n + 1)
                src = bank_a[:, ring_a.bank(step, item)]
                if item[0] == "gram":
                    src = src[:, 0:F]
                else:
                    src = src.rearrange("p (t f) -> p t f", t=HT)
                nc.scalar.copy(dst, src).then_inc(a_taken, 1)

            def take_p(st, i, j, any_before):
                q = i // QT
                if i % QT == 0 and (any_before or q >= 2):
                    act.wait_ge(h_full, j * 4 + (q - 1))
                take(st, ("pT", i, 0), p_t[:, q % 2, 0:HT, (i % QT) * P:(i % QT + 1) * P])

            def prep_xT(step):
                for g in range(2):
                    take(step, ("xT", g), xp_t[:, g * HT:(g + 1) * HT, :])

            def prep_xp(step):
                for g in range(2):
                    take(step, ("xp", g), xp[:, g * HT:(g + 1) * HT, :])

            def prep_gram(step):
                take(step, ("gram", 0), gram[:])

            def prep_xpT(step):
                for g in range(2):
                    take(step, ("xpT", g), xp_t[:, g * HT:(g + 1) * HT, :])

            prep_xT(None)
            prep_xp(None)
            prep_gram(None)
            prep_xpT(None)

            def one_step(st):
                j = st.j
                for i in range(T):
                    if st.own:
                        for hf in range(2):
                            act.wait_ge(score_full, j * (2 * T) + (2 * i + hf + 1))
                            nc.scalar.activation(score[:, i % 2, hf * HN:(hf + 1) * HN], s_ps[:, hf], ACT.Relu,
                                                 scale=SLOPE - 1.0).then_inc(relu_ready, 1)
                        if i > 0:
                            take_p(st, i - 1, j, st.old)
                    if i == 0 and st.old:
                        take_p(st, T - 1, j - 1, True)
                    if st.own:
                        for g in range(2):
                            take(st, ("adjT", i, g), adj_t[:, st.parity, g * HT:(g + 1) * HT, i * P:(i + 1) * P])
                    if i == 1 and st.old:
                        act.wait_ge(d_taken, ring_d.number(st, ("h", 1)) + 1)
                        nc.scalar.activation(exp_h[:], h[:], ACT.Exp).then_inc(exph_ready, 1)
                    if i == 0 and st.next:
                        prep_xT(st)
                    if i == 1 and st.next:
                        prep_xp(st)
                    if i == 2 and st.next:
                        prep_gram(st)
                    if i == 3 and st.next:
                        prep_xpT(st)
                    if st.own:
                        act.wait_ge(negv_ready, j * T + i + 1)
                        nc.scalar.activation(score[:, i % 2], score[:, i % 2], ACT.Exp, scale=-1.0,
                                             bias=neg_max[:, st.parity, i:i + 1],
                                             accum_out=total[:, st.parity, i:i + 1]).then_inc(p_ready, 1)

            steps(act, one_step)

        @block.gpsimd
        def _(pool):
            nc.gpsimd.memset(neg_half[:], -0.5).then_inc(setup, 1)
            nc.gpsimd.memset(ident[:], 0.0).then_inc(setup, 1)
            pool.wait_ge(setup, 2)
            nc.gpsimd.affine_select(out=ident[:], in_=ident[:], compare_op=ALU.not_equal, fill=1.0, base=0,
                                    pattern=[[-1, P]], channel_multiplier=1).then_inc(setup, 1)
            pool.wait_ge(const_in, 64)

            def inverse_norm(step):
                pool.wait_ge(d_taken, ring_d.number(step, ("y", 1)) + 1)
                nc.gpsimd.tensor_tensor(rmag[:], magsq[:], neg_half[:], ALU.pow).then_inc(rmag_ready, 1)

            def inverse_std(dst, src, count, sem_out):
                nc.gpsimd.tensor_scalar(var_eps[:, 0:src.shape[1]], src, EPS, 1.0, ALU.add, ALU.mult
                                        ).then_inc(pool_chain, 1)
                pool.wait_ge(pool_chain, count + 1)
                nc.gpsimd.tensor_tensor(dst, var_eps[:, 0:src.shape[1]], neg_half[:, 0:src.shape[1]], ALU.pow
                                        ).then_inc(sem_out, 1)

            inverse_norm(None)

            def one_step(st):
                j = st.j
                for i in range(T):
                    if st.own:
                        pool.wait_ge(mask_ready, j * T + i + 1)
                        for hf in range(2):
                            pool.wait_ge(relu_ready, j * (2 * T) + (2 * i + hf + 1))
                            cols = slice(hf * HN, (hf + 1) * HN)
                            nc.gpsimd.tensor_tensor(score[:, i % 2, cols], score[:, i % 2, cols],
                                                    maskadd[:, i % 2, cols], ALU.add).then_inc(lrelu_ready, 1)
                    if i == 2 and st.old:
                        pool.wait_ge(stat1_ready, j)
                        hold(pool, "pool")
                        inverse_std(rstd[:], mv[:, :, 1], (j - 1) * 3, rstd1_ready)
                    if i == 4 and st.old:
                        pool.wait_ge(x1_ready, j)
                        nc.gpsimd.tensor_tensor(x1b[:], x1[:], b1_sb[:].unsqueeze(1).broadcast_to([P, T, F]),
                                                ALU.add).then_inc(x1b_ready, 1)
                    if i == 3 and st.next:
                        inverse_norm(st)
                    if i == 5 and st.old:
                        pool.wait_ge(stat2_ready, (j - 1) * 2 + 1)
                        hold(pool, "pool")
                        inverse_std(rstd2[:, 0:HT], mv2[:, 0:HT, 1], (j - 1) * 3 + 1, rstd2_ready)
                    if i == 7 and st.old:
                        pool.wait_ge(stat2_ready, (j - 1) * 2 + 2)
                        hold(pool, "pool")
                        inverse_std(rstd2[:, HT:T], mv2[:, HT:T, 1], (j - 1) * 3 + 2, rstd2_ready)

            steps(pool, one_step)

        @block.vector
        def _(dve):
            LINKS = 5

            def link(ins, n):
                ins.then_inc(dve_chain, 1)
                dve.wait_ge(dve_chain, n)

            def full(step, item):
                dve.wait_ge(d_full, ring_d.number(step, item) + 1)
                return bank_d[:, ring_d.bank(step, item)]

            def row_mask(j, i):
                if i % CH == 0:
                    dve.wait_ge(adj_in[i // CH], (j + 1) * 16)
                nc.vector.tensor_scalar(maskadd[:, i % 2], adj_nat[:, i // CH, i % CH], 0.0, MASKED,
                                        ALU.is_le, ALU.mult).then_inc(mask_ready, 1)

            def negate_and_max(st, i):
                dve.wait_ge(lrelu_ready, st.j * (2 * T) + (2 * i + 2))
                hold(dve, "dve")
                nc.vector.tensor_tensor_reduce(score[:, i % 2], s_ps[:].rearrange("p a n -> p (a n)"), score[:, i % 2],
                                               -1.0, TOP, ALU.add, ALU.min,
                                               neg_max[:, st.parity, i:i + 1]).then_inc(negv_ready, 1)

            def take_p(st, i, j, any_before):
                q = i // QT
                if i % QT == 0 and (any_before or q >= 2):
                    dve.wait_ge(h_full, j * 4 + (q - 1))
                src = full(st, ("pT", i, 1))
                nc.vector.tensor_copy(p_t[:, q % 2, HT:T, (i % QT) * P:(i % QT + 1) * P],
                                      src.rearrange("p (m n) -> p m n", m=HT)).then_inc(d_taken, 1)

            def keep_x(j, parity):
                dve.wait_ge(x_in, (j + 1) * 16)
                nc.vector.tensor_copy(x_nat[:, parity], x_next[:]).then_inc(x_copied, 1)

            def take_h(j, q):
                dve.wait_ge(h_full, j * 4 + (q + 1))
                nc.vector.tensor_copy(h_t[:, q * QN:(q + 1) * QN], h_ps[:, 0:QN]).then_inc(ht_ready, 1)

            def take_u(j, half):
                dve.wait_ge(u_full, j * 2 + half + 1)
                nc.vector.tensor_copy(u_t[:, half * HN:(half + 1) * HN], u_ps[:]).then_inc(ut_ready, 1)

            def norm_squares(step):
                for g in range(2):
                    src = full(step, ("y", g))
                    dve.wait_ge(a_taken, ring_a.number(step, ("xp", g)) + 1)
                    for t in range(HT):
                        r = g * HT + t
                        last = nc.vector.tensor_tensor_reduce(y[:, r, :], src[:, t * F:(t + 1) * F], xp[:, r, :], 1.0, 0.0,
                                                              ALU.mult, ALU.add, magsq[:, r:r + 1])
                    last.then_inc(d_taken, 1)

            def scale_xp(step, j):
                dve.wait_ge(rmag_ready, j + 1)
                for r in range(T):
                    last = nc.vector.tensor_scalar(xp[:, r, :], xp[:, r, :], rmag[:, r:r + 1], None, ALU.mult)
                last.then_inc(xs_ready, 1)

            def split_xsT(step, j, parity):
                for g in range(2):
                    src = full(step, ("xsT", g))
                    cols = slice(g * HN, (g + 1) * HN)
                    nc.vector.tensor_copy(xs_hi[:, parity, cols], src).then_inc(d_hi, 1)
                    dve.wait_ge(d_hi, j * 2 + g + 1)
                    nc.vector.tensor_tensor(xs_lo[:, parity, cols], src, xs_hi[:, parity, cols].bitcast(F32),
                                            ALU.subtract).then_inc(d_taken, 1)

            def normalise(dst, src, mean_var, inv, tiles, done):
                for r in tiles:
                    last = nc.vector.tensor_scalar(dst[:, r, :], src[:, r, :], mean_var[:, r, 0:1], inv[:, r:r + 1],
                                                   ALU.subtract, ALU.mult)
                last.then_inc(done, 1)

            def statistics(src, mean_var, tiles, links, done):
                for r in tiles:
                    last = nc.vector.bn_stats(stats[:, r, :], src[:, r, :])
                last.then_inc(dve_chain, 1)
                dve.wait_ge(dve_chain, links)
                hold(dve, "dve")
                for r in tiles:
                    last = nc.vector.bn_aggr(mean_var[:, r, :], stats[:, r, :])
                last.then_inc(done, 1)

            def finish_layer0(st, j):
                dve.wait_ge(p_ready, j * T + T)
                link(nc.vector.reciprocal(rtotal[:], total[:, 1 - st.parity, :]), j * LINKS + 1)
                for g in range(2):
                    src = full(st, ("h", g))
                    for t in range(HT):
                        r = g * HT + t
                        last = nc.vector.scalar_tensor_tensor(h[:, r, :], src[:, t * F:(t + 1) * F], rtotal[:, r:r + 1],
                                                              b0_sb[:], ALU.mult, ALU.add)
                    last.then_inc(d_taken, 1)

            def add_residual0(st, j, parity):
                dve.wait_ge(d_taken, ring_d.number(st, ("h", 1)) + 1)
                nc.vector.scalar_tensor_tensor(y[:], h[:], 0.0, x_nat[:, parity], ALU.max, ALU.add).then_inc(x_used, 1)
                dve.wait_ge(x_used, j + 1)
                dve.wait_ge(exph_ready, j + 1)
                link(nc.vector.scalar_tensor_tensor(y[:], exp_h[:], 1.0, y[:], ALU.min, ALU.add), j * LINKS + 2)

            def finish_layer1(st, j, half):
                tiles = range(half * HT, (half + 1) * HT)
                src = full(st, ("w", half))
                if half == 0:
                    dve.wait_ge(x1b_ready, j + 1)
                dve.wait_ge(out_done[half], (j + 1) * 16)
                zh = z[:, half * HT:(half + 1) * HT, :]
                nc.vector.tensor_tensor(zh, src.rearrange("p (t f) -> p t f", t=HT), x1b[:, half * HT:(half + 1) * HT, :],
                                        ALU.add).then_inc(d_taken, 1)
                dve.wait_ge(d_taken, ring_d.number(st, ("w", half)) + 1)
                statistics(z, mv2, tiles, j * LINKS + 4 + half, stat2_ready)

            def store_norm(j, half):
                dve.wait_ge(rstd2_ready, j * 2 + half + 1)
                normalise(z, z, mv2, rstd2, range(half * HT, (half + 1) * HT), out_ready)

            for half in range(2):
                nc.vector.memset(z[:, half * HT, 0:1], 0.0).then_inc(out_done[half], 16)
            dve.wait_ge(const_in, 64)
            keep_x(0, 0)
            norm_squares(None)
            row_mask(0, 0)
            scale_xp(None, 0)
            split_xsT(None, 0, 0)

            def one_step(st):
                j = st.j
                for i in range(T):
                    if i > 0 and st.own:
                        take_p(st, i - 1, j, st.old)
                    if st.old:
                        if i == 0:
                            take_p(st, T - 1, j - 1, True)
                        if i == 2:
                            statistics(y, mv, range(T), (j - 1) * LINKS + 3, stat1_ready)
                        if i == 3:
                            dve.wait_ge(rstd1_ready, j)
                            normalise(x1, y, mv, rstd, range(T), x1_ready)
                    if st.own:
                        if i + 1 < T:
                            row_mask(j, i + 1)
                        elif st.next:
                            row_mask(j + 1, 0)
                        negate_and_max(st, i)
                    if i == 0 and st.old:
                        take_h(j - 1, 3)
                        finish_layer0(st, j - 1)
                    if i == 1 and st.old:
                        add_residual0(st, j - 1, 1 - st.parity)
                    if i == 2:
                        if st.next:
                            keep_x(j + 1, 1 - st.parity)
                        if st.own:
                            take_h(j, 0)
                    if i == 3 and st.next:
                        if st.old:
                            dve.wait_ge(x1_ready, j)
                        norm_squares(st)
                    if i == 4:
                        if st.next:
                            scale_xp(st, j + 1)
                        if st.own:
                            take_h(j, 1)
                        if st.old:
                            take_u(j - 1, 0)
                    if i == 5:
                        if st.next:
                            split_xsT(st, j + 1, 1 - st.parity)
                        if st.old:
                            finish_layer1(st, j - 1, 0)
                    if i == 6 and st.old:
                        store_norm(j - 1, 0)
                        take_u(j - 1, 1)
                    if i == 7:
                        if st.old:
                            finish_layer1(st, j - 1, 1)
                        if st.own:
                            take_h(j, 2)
                        if st.old:
                            store_norm(j - 1, 1)

            steps(dve, one_step)


_INS = ["x", "adj", "L0_gnn_W_a", "L0_gnn_bias", "L1_gnn_weight", "L1_gnn_bias"]
_OUTS = [((8, 1024, 128), "float32")]


def kernel(**inputs):
    import numpy as _np
    import concourse.bacc as _bacc
    from concourse import mybir as _mybir
    from concourse.bass_utils import run_bass_kernel_spmd as _run

    nc = _bacc.Bacc("TRN2", target_bir_lowering=False, num_devices=1)
    arrays, args = {}, []
    for name in _INS:
        a = _np.ascontiguousarray(inputs[name])
        arrays[f"in_{name}_dram"] = a
        args.append(nc.dram_tensor(f"in_{name}_dram", a.shape, _mybir.dt.from_np(a.dtype), kind="ExternalInput").ap())
    for i, (shape, dtype) in enumerate(_OUTS):
        dt = _mybir.dt.from_np(_np.dtype(dtype))
        args.append(nc.dram_tensor(f"out_{i}_dram", shape, dt, kind="ExternalOutput").ap())
    gnn_kernel(nc, *args)
    r = _run(nc, [arrays], core_ids=[0])
    return r.results[0]["out_0_dram"]
```

```python
from contextlib import ExitStack

import concourse.bass as bass
from concourse import mybir

F32 = mybir.dt.float32
F32R = mybir.dt.float32r
BF16 = mybir.dt.bfloat16
ALU = mybir.AluOpType
ACT = mybir.ActivationFunctionType

P = 128
SLOPE = -0.2
MASKED = -2.0 ** 126
TOP = 3.0e38
EPS = 1e-5
OLD, NEXT, OWN = "old", "next", "own"


class Step:

    def __init__(self, j, parity, old=True, next=True, own=True):
        self.j, self.parity, self.old, self.next, self.own = j, parity, old, next, own


class Ring:

    def __init__(self, plan):
        self.plan = plan
        self.first = [item for part, item in plan if part == NEXT]
        self.old = sum(part == OLD for part, _ in plan)

    def begin(self, step):
        if not step.old:
            return len(self.first)
        lacking = self.old if step.own else self.old + len(self.first)
        return step.j * len(self.plan) + (len(self.first) - lacking)

    def number(self, step, item):
        if step is None:
            return self.first.index(item)
        has = {OWN: step.own, OLD: step.old, NEXT: step.next}
        return self.begin(step) + [it for part, it in self.plan if has[part]].index(item)

    def bank(self, step, item):
        if step is None:
            return self.number(None, item) % 2
        return self.number(Step(step.parity, step.parity, step.old, step.next, step.own), item) % 2


def gnn_kernel(nc, x, adj, w_a, bias0, weight, bias1, out):
    B, N, F = x.shape
    T = N // P
    HT = T // 2
    HN = N // 2
    QT = T // 4
    QN = N // 4
    CH = 2
    NCH = T // CH

    plan_a = []
    plan_d = []
    for i in range(T):
        for plan, g in ((plan_a, 0), (plan_d, 1)):
            plan += [(OLD, ("pT", T - 1, g)) if i == 0 else (OWN, ("pT", i - 1, g))]
        plan_a += [(OWN, ("adjT", i, g)) for g in range(2)]
        if i == 0:
            plan_a += [(NEXT, ("xT", g)) for g in range(2)]
            plan_d += [(OLD, ("h", 1))]
        if i == 1:
            plan_a += [(NEXT, ("xp", g)) for g in range(2)]
        if i == 2:
            plan_a += [(NEXT, ("gram", 0))]
        if i == 3:
            plan_a += [(NEXT, ("xpT", g)) for g in range(2)]
            plan_d += [(NEXT, ("y", g)) for g in range(2)]
        if i == 4:
            plan_d += [(OLD, ("w", 0))]
        if i == 5:
            plan_d += [(NEXT, ("xsT", g)) for g in range(2)]
            plan_d += [(OWN, ("h", 0))]
        if i == 7:
            plan_d += [(OLD, ("w", 1))]
    ring_a, ring_d = Ring(plan_a), Ring(plan_d)

    with ExitStack() as ctx:
        def sb(name, shape, dt=F32):
            return ctx.enter_context(nc.sbuf_tensor(name, shape, dt))

        def psum(name, shape, dt=F32):
            return ctx.enter_context(nc.psum_tensor(name, shape, dt))

        def sem(name):
            return ctx.enter_context(nc.semaphore(name))

        adj_nat = sb("adj_nat", [P, NCH, CH, N])
        adj_t = sb("adj_t", [P, 2, T, N])
        p_t = sb("p_t", [P, 2, T, QN])
        score = sb("score", [P, 2, N])
        maskadd = sb("maskadd", [P, 2, N], BF16)
        x_next = sb("x_next", [P, T, F])
        x_nat = sb("x_nat", [P, 2, T, F])
        xp_t = sb("xp_t", [P, T, P])
        xp = sb("xp", [P, T, F])
        gram = sb("gram", [P, F])
        xs_hi = sb("xs_hi", [P, 2, N], F32R)
        xs_lo = sb("xs_lo", [P, 2, N], F32R)
        h_t = sb("h_t", [P, N])
        h = sb("h", [P, T, F])
        exp_h = sb("exp_h", [P, T, F])
        u_t = exp_h[:].rearrange("p t f -> p (t f)")
        y = sb("y", [P, T, F])
        x1 = sb("x1", [P, T, F])
        x1b = sb("x1b", [P, T, F])
        z = sb("z", [P, T, F])
        stats = sb("stats", [P, T, 6])
        mv = sb("mv", [P, T, 2])
        mv2 = sb("mv2", [P, T, 2])
        var_eps = sb("var_eps", [P, 2, T])
        rstd = sb("rstd", [P, T])
        rstd2 = sb("rstd2", [P, T])
        magsq = sb("magsq", [P, T])
        rmag = sb("rmag", [P, T])
        neg_max = sb("neg_max", [P, 2, T])
        neg_part = sb("neg_part", [P, 2])
        total = sb("total", [P, 2, T])
        rtotal = sb("rtotal", [P, T])
        neg_half = sb("neg_half", [P, T])
        ident = sb("ident", [P, P])
        wa_sb = sb("wa_sb", [F, F])
        w1_sb = sb("w1_sb", [F, F])
        b0_sb = sb("b0_sb", [P, F])
        b1_sb = sb("b1_sb", [P, F])

        s_ps = psum("s_ps", [P, 2, 512])
        bank_a = psum("bank_a", [P, 2, 512])
        bank_d = psum("bank_d", [P, 2, 512])
        h_ps = psum("h_ps", [P, 512])
        u_ps = psum("u_ps", [P, 512])

        const_in = sem("const_in")
        adj_in = [sem(f"adj_in{c}") for c in range(NCH)]
        x_in = [sem(f"x_in{g}") for g in range(2)]
        x_copied = sem("x_copied")
        out_done = [sem(f"out_done{c}") for c in range(2)]
        setup = sem("setup")
        a_full, a_taken = sem("a_full"), sem("a_taken")
        d_full, d_taken = sem("d_full"), sem("d_taken")
        xs_hi_ready = sem("xs_hi_ready")
        score_full = sem("score_full")
        relu_ready = sem("relu_ready")
        mask_ready = sem("mask_ready")
        lrelu_ready = sem("lrelu_ready")
        negv_half, negv_ready = sem("negv_half"), sem("negv_ready")
        p_ready = sem("p_ready")
        h_full, ht_ready = sem("h_full"), sem("ht_ready")
        u_full, ut_ready = sem("u_full"), sem("ut_ready")
        exph_ready = sem("exph_ready")
        x_used = sem("x_used")
        stat1_ready, rstd1_ready = sem("stat1_ready"), sem("rstd1_ready")
        x1_ready, x1b_ready = sem("x1_ready"), sem("x1b_ready")
        stat2_ready, rstd2_ready = sem("stat2_ready"), sem("rstd2_ready")
        out_ready = sem("out_ready")
        rmag_ready, xs_ready = sem("rmag_ready"), sem("xs_ready")
        rtotal_ready, y_ready = sem("rtotal_ready"), sem("y_ready")
        half_stats1, half_stats2 = sem("half_stats1"), sem("half_stats2")
        eps1_ready, eps2_ready = sem("eps1_ready"), sem("eps2_ready")

        def steps(eng, one_step):
            one_step(Step(0, 0, old=False))
            with eng.Fori(0, (B - 2) // 2) as k:
                for u in range(2):
                    one_step(Step(k * 2 + (1 + u), (1 + u) % 2))
            one_step(Step(B - 1, (B - 1) % 2, next=False))
            one_step(Step(B, B % 2, next=False, own=False))

        met = {"sp": sem("met_sp"), "pool": sem("met_pool"), "dve": sem("met_dve")}

        def hold(eng, name):
            eng.sem_inc(met[name], 1)

        def u_bank(half, own):
            return u_ps if own or half == 0 else h_ps

        block = ctx.enter_context(nc.Block())

        @block.sync
        def _(sp):
            def load_adj(c, j):
                sp.dma_start(adj_nat[:, c], adj[j, c * CH * P:(c + 1) * CH * P, :].rearrange("(t p) m -> p t m", p=P)
                             ).then_inc(adj_in[c], 16)

            def load_x(j):
                for g in range(2):
                    sp.dma_start(x_next[:, g * HT:(g + 1) * HT], x[j, g * HN:(g + 1) * HN, :]
                                 .rearrange("(t p) f -> p t f", p=P)).then_inc(x_in[g], 16)

            load_x(0)
            sp.dma_start(wa_sb[:], w_a).then_inc(const_in, 16)
            sp.dma_start(w1_sb[:], weight).then_inc(const_in, 16)
            sp.dma_start(b0_sb[:], bias0.broadcast_to([P, F])).then_inc(const_in, 16)
            sp.dma_start(b1_sb[:], bias1.rearrange("(a f) -> a f", a=1).broadcast_to([P, F])).then_inc(const_in, 16)
            for c in range(NCH):
                load_adj(c, 0)

            def one_step(st):
                if st.next:
                    sp.wait_ge(a_full, ring_a.begin(st))
                    hold(sp, "sp")
                    sp.wait_ge(x_copied, st.j + 1)
                    hold(sp, "sp")
                    load_x(st.j + 1)
                for c in range(NCH):
                    if st.next:
                        sp.wait_ge(a_full, ring_a.number(st, ("adjT", CH * c + CH - 1, 1)) + 1)
                        hold(sp, "sp")
                        sp.wait_ge(mask_ready, st.j * T + CH * (c + 1))
                        hold(sp, "sp")
                        load_adj(c, st.j + 1)
                if st.old:
                    for half in range(2):
                        sp.wait_ge(out_ready, (st.j - 1) * 2 + half + 1)
                        hold(sp, "sp")
                        sp.dma_start(out[st.j - 1, half * HN:(half + 1) * HN, :].rearrange("(t p) f -> p t f", p=P),
                                     z[:, half * HT:(half + 1) * HT]).then_inc(out_done[half], 16)

            steps(sp, one_step)
            for half in range(2):
                sp.wait_ge(out_done[half], 16 * (B + 1))

        @block.tensor
        def _(pe):
            def open_a(step, item):
                n = ring_a.number(step, item)
                if step is not None or n >= 2:
                    pe.wait_ge(a_taken, n - 1)
                return bank_a[:, ring_a.bank(step, item)]

            def open_d(step, item):
                n = ring_d.number(step, item)
                if step is not None or n >= 2:
                    pe.wait_ge(d_taken, n - 1)
                return bank_d[:, ring_d.bank(step, item)]

            def prep_xT(step, j):
                for g in range(2):
                    dst = open_a(step, ("xT", g))
                    pe.wait_ge(x_in[g], (j + 1) * 16)
                    for t in range(HT):
                        mm = pe.transpose(dst[:, t * P:(t + 1) * P], x_next[:, g * HT + t, :], ident[:])
                    mm.then_inc(a_full, 1)

            def prep_xp(step):
                for g in range(2):
                    dst = open_a(step, ("xp", g))
                    pe.wait_ge(a_taken, ring_a.number(step, ("xT", g)) + 1)
                    for t in range(HT):
                        mm = pe.matmul(dst[:, t * F:(t + 1) * F], xp_t[:, g * HT + t, :], wa_sb[:], start=True, stop=True)
                    mm.then_inc(a_full, 1)

            def prep_gram(step):
                dst = open_a(step, ("gram", 0))
                pe.wait_ge(a_taken, ring_a.number(step, ("xp", 1)) + 1)
                for t in range(T):
                    mm = pe.matmul(dst[:, 0:F], xp[:, t, :], xp[:, t, :], start=(t == 0), stop=(t == T - 1))
                mm.then_inc(a_full, 1)

            def prep_xpT(step):
                for g in range(2):
                    dst = open_a(step, ("xpT", g))
                    for t in range(HT):
                        mm = pe.transpose(dst[:, t * P:(t + 1) * P], xp[:, g * HT + t, :], ident[:])
                    mm.then_inc(a_full, 1)

            def prep_y(step):
                for g in range(2):
                    dst = open_d(step, ("y", g))
                    pe.wait_ge(a_taken, ring_a.number(step, ("xpT", g)) + 1)
                    for t in range(HT):
                        mm = pe.matmul(dst[:, t * F:(t + 1) * F], xp_t[:, g * HT + t, :], gram[:], start=True, stop=True)
                    mm.then_inc(d_full, 1)

            def prep_xsT(step, j):
                for g in range(2):
                    dst = open_d(step, ("xsT", g))
                    pe.wait_ge(xs_ready, j * 2 + (g + 1))
                    for t in range(HT):
                        mm = pe.transpose(dst[:, t * P:(t + 1) * P], xp[:, g * HT + t, :], ident[:])
                    mm.then_inc(d_full, 1)

            def transpose_adj(st, i):
                for g in range(2):
                    dst = open_a(st, ("adjT", i, g))
                    for m in range(HT):
                        col = (g * HT + m) * P
                        mm = pe.transpose(dst[:, m * P:(m + 1) * P], adj_nat[:, i // CH, i % CH, col:col + P], ident[:])
                    mm.then_inc(a_full, 1)

            def scores(st, i, j):
                if i == 0:
                    pe.wait_ge(d_taken, ring_d.begin(st) - (2 if st.old else 0))
                rows = slice(i * P, (i + 1) * P)
                for hf in range(2):
                    cols = slice(hf * HN, (hf + 1) * HN)
                    if st.old or i > 0:
                        pe.wait_ge((negv_half, negv_ready)[hf], j * T + i)
                    hi, lo = xs_hi[:, st.parity], xs_lo[:, st.parity]
                    pe.matmul(s_ps[:, hf], hi[:, rows], hi[:, cols], start=True, stop=False)
                    pe.matmul(s_ps[:, hf], hi[:, rows], lo[:, cols], start=False, stop=False)
                    pe.matmul(s_ps[:, hf], lo[:, rows], hi[:, cols], start=False, stop=True).then_inc(score_full, 1)

            def transpose_p(st, i, j):
                pe.wait_ge(p_ready, j * T + i + 1)
                for g, (opened, filled) in enumerate(((open_a, a_full), (open_d, d_full))):
                    dst = opened(st, ("pT", i, g))
                    for m in range(HT):
                        col = (g * HT + m) * P
                        mm = pe.transpose(dst[:, m * P:(m + 1) * P], score[:, i % 2, col:col + P], ident[:])
                    mm.then_inc(filled, 1)

            def attend(st, q, j, parity, any_before):
                pe.wait_ge(a_taken, ring_a.number(st, ("pT", q * QT + QT - 1, 0)) + 1)
                pe.wait_ge(d_taken, ring_d.number(st, ("pT", q * QT + QT - 1, 1)) + 1)
                if any_before:
                    pe.wait_ge(ht_ready, j * 4 + q)
                if q == 0:
                    pe.wait_ge(x_copied, j + 1)
                for m in range(T):
                    mm = pe.matmul(h_ps[:, 0:QN], x_nat[:, parity, m, :], p_t[:, q % 2, m, :],
                                   start=(m == 0), stop=(m == T - 1))
                mm.then_inc(h_full, 1)

            def transpose_h(st, j, g):
                pe.wait_ge(ht_ready, j * 4 + 2 * g + 2)
                dst = open_d(st, ("h", g))
                for t in range(HT):
                    mm = pe.transpose(dst[:, t * P:(t + 1) * P], h_t[:, (g * HT + t) * P:(g * HT + t + 1) * P], ident[:])
                mm.then_inc(d_full, 1)

            def aggregate(j, parity, half, m0, m1, own=True):
                pe.wait_ge(x1_ready, j * 2 + m1 // HT)
                if m0 == 0 and half == 1 and own:
                    pe.wait_ge(ut_ready, j * 2 + 1)
                for m in range(m0, m1):
                    mm = pe.matmul(u_bank(half, own)[:], x1[:, m, :], adj_t[:, parity, m, half * HN:(half + 1) * HN],
                                   start=(m == 0), stop=(m == T - 1))
                if m1 == T:
                    mm.then_inc(u_full, 1)

            def project(st, j, half):
                dst = open_d(st, ("w", half))
                pe.wait_ge(ut_ready, j * 2 + half + 1)
                for t in range(HT):
                    col = (half * HT + t) * P
                    mm = pe.matmul(dst[:, t * F:(t + 1) * F], u_t[:, col:col + P], w1_sb[:], start=True, stop=True)
                mm.then_inc(d_full, 1)

            pe.wait_ge(setup, 3)
            prep_xT(None, 0)
            pe.wait_ge(const_in, 64)
            prep_xp(None)
            prep_gram(None)
            prep_xpT(None)
            prep_y(None)
            prep_xsT(None, 0)

            def one_step(st):
                j = st.j
                for i in range(T):
                    if st.own:
                        scores(st, i, j)
                        if i > 0:
                            transpose_p(st, i - 1, j)
                    if i == 0 and st.old:
                        transpose_p(st, T - 1, j - 1)
                    if st.own:
                        if i % CH == 0:
                            pe.wait_ge(adj_in[i // CH], (j + 1) * 16)
                        transpose_adj(st, i)
                    if i == 0:
                        if st.old:
                            attend(st, 3, j - 1, 1 - st.parity, True)
                        if st.next:
                            prep_xT(st, j + 1)
                        if st.old:
                            transpose_h(st, j - 1, 1)
                    if i == 1:
                        if st.next:
                            prep_xp(st)
                        if st.old:
                            aggregate(j - 1, 1 - st.parity, 0, 0, HT)
                            if not st.own:
                                aggregate(j - 1, 1 - st.parity, 1, 0, HT, own=False)
                    if i == 2:
                        if st.next:
                            prep_gram(st)
                        if st.own:
                            attend(st, 0, j, st.parity, st.old)
                    if i == 3:
                        if st.next:
                            prep_xpT(st)
                            prep_y(st)
                        if st.old:
                            aggregate(j - 1, 1 - st.parity, 0, HT, T)
                            if not st.own:
                                aggregate(j - 1, 1 - st.parity, 1, HT, T, own=False)
                    if i == 4:
                        if st.own:
                            attend(st, 1, j, st.parity, True)
                        if st.old:
                            project(st, j - 1, 0)
                    if i == 5:
                        if st.next:
                            prep_xsT(st, j + 1)
                        if st.old and st.own:
                            aggregate(j - 1, 1 - st.parity, 1, 0, HT)
                        if st.own:
                            transpose_h(st, j, 0)
                    if i == 6 and st.old and st.own:
                        aggregate(j - 1, 1 - st.parity, 1, HT, T)
                    if i == 7:
                        if st.old:
                            project(st, j - 1, 1)
                        if st.own:
                            attend(st, 2, j, st.parity, True)

            steps(pe, one_step)

        @block.scalar
        def _(act):
            def take(step, item, dst):
                n = ring_a.number(step, item)
                act.wait_ge(a_full, n + 1)
                src = bank_a[:, ring_a.bank(step, item)]
                if item[0] == "gram":
                    src = src[:, 0:F]
                else:
                    src = src.rearrange("p (t f) -> p t f", t=HT)
                nc.scalar.copy(dst, src).then_inc(a_taken, 1)

            def take_p(st, i, j, any_before):
                q = i // QT
                if i % QT == 0 and (any_before or q >= 2):
                    act.wait_ge(h_full, j * 4 + (q - 1))
                take(st, ("pT", i, 0), p_t[:, q % 2, 0:HT, (i % QT) * P:(i % QT + 1) * P])

            def prep_xT(step):
                for g in range(2):
                    take(step, ("xT", g), xp_t[:, g * HT:(g + 1) * HT, :])

            def prep_xp(step):
                for g in range(2):
                    take(step, ("xp", g), xp[:, g * HT:(g + 1) * HT, :])

            def exp_of_h(st, g):
                act.wait_ge(d_taken, ring_d.number(st, ("h", g)) + 1)
                nc.scalar.activation(exp_h[:, g * HT:(g + 1) * HT], h[:, g * HT:(g + 1) * HT], ACT.Exp
                                     ).then_inc(exph_ready, 1)

            def high_xsT(step, parity):
                for g in range(2):
                    act.wait_ge(d_full, ring_d.number(step, ("xsT", g)) + 1)
                    nc.scalar.copy(xs_hi[:, parity, g * HN:(g + 1) * HN], bank_d[:, ring_d.bank(step, ("xsT", g))]
                                   ).then_inc(xs_hi_ready, 1)

            def prep_gram(step):
                take(step, ("gram", 0), gram[:])

            def prep_xpT(step):
                for g in range(2):
                    take(step, ("xpT", g), xp_t[:, g * HT:(g + 1) * HT, :])

            prep_xT(None)
            prep_xp(None)
            prep_gram(None)
            prep_xpT(None)
            high_xsT(None, 0)

            def one_step(st):
                j = st.j
                for i in range(T):
                    if st.own:
                        for hf in range(2):
                            act.wait_ge(score_full, j * (2 * T) + (2 * i + hf + 1))
                            nc.scalar.activation(score[:, i % 2, hf * HN:(hf + 1) * HN], s_ps[:, hf], ACT.Relu,
                                                 scale=SLOPE - 1.0).then_inc(relu_ready, 1)
                        if i > 0:
                            take_p(st, i - 1, j, st.old)
                    if i == 0 and st.old:
                        take_p(st, T - 1, j - 1, True)
                    if st.own:
                        for g in range(2):
                            take(st, ("adjT", i, g), adj_t[:, st.parity, g * HT:(g + 1) * HT, i * P:(i + 1) * P])
                    if i == 1 and st.old:
                        exp_of_h(st, 1)
                    if i == 6 and st.own:
                        exp_of_h(st, 0)
                    if i == 0 and st.next:
                        prep_xT(st)
                    if i == 1 and st.next:
                        prep_xp(st)
                    if i == 2 and st.next:
                        prep_gram(st)
                    if i == 3 and st.next:
                        prep_xpT(st)
                    if i == 5 and st.next:
                        high_xsT(st, 1 - st.parity)
                    if st.own:
                        act.wait_ge(negv_ready, j * T + i + 1)
                        nc.scalar.activation(score[:, i % 2], score[:, i % 2], ACT.Exp, scale=-1.0,
                                             bias=neg_max[:, st.parity, i:i + 1],
                                             accum_out=total[:, st.parity, i:i + 1]).then_inc(p_ready, 1)

            steps(act, one_step)

        @block.gpsimd
        def _(pool):
            nc.gpsimd.memset(neg_half[:], -0.5).then_inc(setup, 1)
            nc.gpsimd.memset(ident[:], 0.0).then_inc(setup, 1)
            pool.wait_ge(setup, 2)
            nc.gpsimd.affine_select(out=ident[:], in_=ident[:], compare_op=ALU.not_equal, fill=1.0, base=0,
                                    pattern=[[-1, P]], channel_multiplier=1).then_inc(setup, 1)
            pool.wait_ge(const_in, 64)

            def inverse_norm(step):
                for g in range(2):
                    tiles = slice(g * HT, (g + 1) * HT)
                    pool.wait_ge(d_taken, ring_d.number(step, ("y", g)) + 1)
                    nc.gpsimd.tensor_tensor(rmag[:, tiles], magsq[:, tiles], neg_half[:, tiles], ALU.pow
                                            ).then_inc(rmag_ready, 1)

            def inverse_std(stat_ready, eps_ready, done, layer, mean_var, dst, j, g):
                tiles = slice(g * HT, (g + 1) * HT)
                pool.wait_ge(stat_ready, j * 2 + (g + 1))
                hold(pool, "pool")
                nc.gpsimd.tensor_scalar(var_eps[:, layer, tiles], mean_var[:, tiles, 1], EPS, 1.0, ALU.add, ALU.mult
                                        ).then_inc(eps_ready, 1)
                pool.wait_ge(eps_ready, j * 2 + (g + 1))
                nc.gpsimd.tensor_tensor(dst[:, tiles], var_eps[:, layer, tiles], neg_half[:, tiles], ALU.pow
                                        ).then_inc(done, 1)

            inverse_norm(None)

            def one_step(st):
                j = st.j
                for i in range(T):
                    if st.own:
                        pool.wait_ge(mask_ready, j * T + i + 1)
                        for hf in range(2):
                            pool.wait_ge(relu_ready, j * (2 * T) + (2 * i + hf + 1))
                            cols = slice(hf * HN, (hf + 1) * HN)
                            nc.gpsimd.tensor_tensor(score[:, i % 2, cols], score[:, i % 2, cols],
                                                    maskadd[:, i % 2, cols], ALU.add).then_inc(lrelu_ready, 1)
                    if i == 2 and st.old:
                        inverse_std(stat1_ready, eps1_ready, rstd1_ready, 0, mv, rstd, j - 1, 1)
                    if i == 3:
                        if st.old:
                            pool.wait_ge(x1_ready, j * 2)
                            nc.gpsimd.tensor_tensor(x1b[:], x1[:], b1_sb[:].unsqueeze(1).broadcast_to([P, T, F]),
                                                    ALU.add).then_inc(x1b_ready, 1)
                        if st.next:
                            inverse_norm(st)
                    if i == 5 and st.old:
                        inverse_std(stat2_ready, eps2_ready, rstd2_ready, 1, mv2, rstd2, j - 1, 0)
                    if i == 7:
                        if st.own:
                            inverse_std(stat1_ready, eps1_ready, rstd1_ready, 0, mv, rstd, j, 0)
                        if st.old:
                            inverse_std(stat2_ready, eps2_ready, rstd2_ready, 1, mv2, rstd2, j - 1, 1)

            steps(pool, one_step)

        @block.vector
        def _(dve):
            def full(step, item):
                dve.wait_ge(d_full, ring_d.number(step, item) + 1)
                return bank_d[:, ring_d.bank(step, item)]

            def row_mask(j, i):
                if i % CH == 0:
                    dve.wait_ge(adj_in[i // CH], (j + 1) * 16)
                nc.vector.tensor_scalar(maskadd[:, i % 2], adj_nat[:, i // CH, i % CH], 0.0, MASKED,
                                        ALU.is_le, ALU.mult).then_inc(mask_ready, 1)

            def negate_and_max(st, i):
                low = (neg_part[:, i % 2:i % 2 + 1], neg_max[:, st.parity, i:i + 1])
                for hf in range(2):
                    cols = slice(hf * HN, (hf + 1) * HN)
                    dve.wait_ge(lrelu_ready, st.j * (2 * T) + (2 * i + hf + 1))
                    if hf == 1:
                        dve.wait_ge(negv_half, st.j * T + (i + 1))
                    hold(dve, "dve")
                    nc.vector.tensor_tensor_reduce(score[:, i % 2, cols], s_ps[:, hf], score[:, i % 2, cols],
                                                   -1.0, (TOP, low[0])[hf], ALU.add, ALU.min, low[hf]
                                                   ).then_inc((negv_half, negv_ready)[hf], 1)

            def take_p(st, i, j, any_before):
                q = i // QT
                if i % QT == 0 and (any_before or q >= 2):
                    dve.wait_ge(h_full, j * 4 + (q - 1))
                src = full(st, ("pT", i, 1))
                nc.vector.tensor_copy(p_t[:, q % 2, HT:T, (i % QT) * P:(i % QT + 1) * P],
                                      src.rearrange("p (m n) -> p m n", m=HT)).then_inc(d_taken, 1)

            def keep_x(j, parity):
                for g in range(2):
                    dve.wait_ge(x_in[g], (j + 1) * 16)
                nc.vector.tensor_copy(x_nat[:, parity], x_next[:]).then_inc(x_copied, 1)

            def take_h(j, q):
                dve.wait_ge(h_full, j * 4 + (q + 1))
                nc.vector.tensor_copy(h_t[:, q * QN:(q + 1) * QN], h_ps[:, 0:QN]).then_inc(ht_ready, 1)

            def take_u(j, half, own):
                dve.wait_ge(u_full, j * 2 + half + 1)
                nc.vector.tensor_copy(u_t[:, half * HN:(half + 1) * HN], u_bank(half, own)[:]).then_inc(ut_ready, 1)

            def norm_squares(step):
                for g in range(2):
                    src = full(step, ("y", g))
                    dve.wait_ge(a_taken, ring_a.number(step, ("xp", g)) + 1)
                    for t in range(HT):
                        r = g * HT + t
                        last = nc.vector.tensor_tensor_reduce(y[:, r, :], src[:, t * F:(t + 1) * F], xp[:, r, :], 1.0, 0.0,
                                                              ALU.mult, ALU.add, magsq[:, r:r + 1])
                    last.then_inc(d_taken, 1)

            def scale_xp(step, j):
                for g in range(2):
                    dve.wait_ge(rmag_ready, j * 2 + (g + 1))
                    for r in range(g * HT, (g + 1) * HT):
                        last = nc.vector.tensor_scalar(xp[:, r, :], xp[:, r, :], rmag[:, r:r + 1], None, ALU.mult)
                    last.then_inc(xs_ready, 1)

            def split_xsT(step, j, parity):
                for g in range(2):
                    dve.wait_ge(xs_hi_ready, j * 2 + g + 1)
                    src = bank_d[:, ring_d.bank(step, ("xsT", g))]
                    cols = slice(g * HN, (g + 1) * HN)
                    nc.vector.tensor_tensor(xs_lo[:, parity, cols], src, xs_hi[:, parity, cols].bitcast(F32),
                                            ALU.subtract).then_inc(d_taken, 1)

            def normalise(dst, src, mean_var, inv, tiles, done):
                for r in tiles:
                    last = nc.vector.tensor_scalar(dst[:, r, :], src[:, r, :], mean_var[:, r, 0:1], inv[:, r:r + 1],
                                                   ALU.subtract, ALU.mult)
                last.then_inc(done, 1)

            def statistics(src, mean_var, g, j, raw, done):
                tiles = range(g * HT, (g + 1) * HT)
                for r in tiles:
                    last = nc.vector.bn_stats(stats[:, r, :], src[:, r, :])
                last.then_inc(raw, 1)
                dve.wait_ge(raw, j * 2 + (g + 1))
                hold(dve, "dve")
                for r in tiles:
                    last = nc.vector.bn_aggr(mean_var[:, r, :], stats[:, r, :])
                last.then_inc(done, 1)

            def finish_attention(st, j, g, parity):
                dve.wait_ge(p_ready, j * T + (g + 1) * HT)
                tiles = slice(g * HT, (g + 1) * HT)
                nc.vector.reciprocal(rtotal[:, tiles], total[:, parity, tiles]).then_inc(rtotal_ready, 1)
                src = full(st, ("h", g))
                dve.wait_ge(rtotal_ready, j * 2 + (g + 1))
                for t in range(HT):
                    r = g * HT + t
                    last = nc.vector.scalar_tensor_tensor(h[:, r, :], src[:, t * F:(t + 1) * F], rtotal[:, r:r + 1],
                                                          b0_sb[:], ALU.mult, ALU.add)
                last.then_inc(d_taken, 1)

            def add_residual0(st, j, g, parity):
                tiles = slice(g * HT, (g + 1) * HT)
                dve.wait_ge(d_taken, ring_d.number(st, ("h", g)) + 1)
                nc.vector.scalar_tensor_tensor(y[:, tiles], h[:, tiles], 0.0, x_nat[:, parity, tiles], ALU.max, ALU.add
                                               ).then_inc(x_used, 1)
                dve.wait_ge(x_used, j * 2 + (g + 1))
                dve.wait_ge(exph_ready, j * 2 + (g + 1))
                nc.vector.scalar_tensor_tensor(y[:, tiles], exp_h[:, tiles], 1.0, y[:, tiles], ALU.min, ALU.add
                                               ).then_inc(y_ready, 1)
                dve.wait_ge(y_ready, j * 2 + (g + 1))

            def layer_norm0(j, g):
                dve.wait_ge(rstd1_ready, j * 2 + (g + 1))
                normalise(x1, y, mv, rstd, range(g * HT, (g + 1) * HT), x1_ready)

            def finish_layer1(st, j, half):
                src = full(st, ("w", half))
                if half == 0:
                    dve.wait_ge(x1b_ready, j + 1)
                dve.wait_ge(out_done[half], (j + 1) * 16)
                zh = z[:, half * HT:(half + 1) * HT, :]
                nc.vector.tensor_tensor(zh, src.rearrange("p (t f) -> p t f", t=HT), x1b[:, half * HT:(half + 1) * HT, :],
                                        ALU.add).then_inc(d_taken, 1)
                dve.wait_ge(d_taken, ring_d.number(st, ("w", half)) + 1)
                statistics(z, mv2, half, j, half_stats2, stat2_ready)

            def store_norm(j, half):
                dve.wait_ge(rstd2_ready, j * 2 + half + 1)
                normalise(z, z, mv2, rstd2, range(half * HT, (half + 1) * HT), out_ready)

            for half in range(2):
                nc.vector.memset(z[:, half * HT, 0:1], 0.0).then_inc(out_done[half], 16)
            dve.wait_ge(const_in, 64)
            norm_squares(None)
            scale_xp(None, 0)
            row_mask(0, 0)
            split_xsT(None, 0, 0)
            keep_x(0, 0)

            def one_step(st):
                j = st.j
                for i in range(T):
                    if i > 0 and st.own:
                        take_p(st, i - 1, j, st.old)
                    if i == 0 and st.old:
                        take_p(st, T - 1, j - 1, True)
                    if i == 2 and st.old:
                        statistics(y, mv, 1, j - 1, half_stats1, stat1_ready)
                    if i == 3 and st.old:
                        layer_norm0(j - 1, 1)
                    if st.own:
                        if i + 1 < T:
                            row_mask(j, i + 1)
                        elif st.next:
                            row_mask(j + 1, 0)
                        negate_and_max(st, i)
                    if i == 0 and st.old:
                        layer_norm0(j - 1, 0)
                        take_h(j - 1, 3)
                        finish_attention(st, j - 1, 1, 1 - st.parity)
                    if i == 1 and st.old:
                        add_residual0(st, j - 1, 1, 1 - st.parity)
                    if i == 2:
                        if st.next:
                            keep_x(j + 1, 1 - st.parity)
                        if st.own:
                            take_h(j, 0)
                    if i == 3 and st.next:
                        if st.old:
                            dve.wait_ge(x1_ready, j * 2)
                        norm_squares(st)
                    if i == 4:
                        if st.old:
                            take_u(j - 1, 0, st.own)
                            if not st.own:
                                take_u(j - 1, 1, False)
                        if st.next:
                            scale_xp(st, j + 1)
                        if st.own:
                            take_h(j, 1)
                        if st.old:
                            finish_layer1(st, j - 1, 0)
                    if i == 5:
                        if st.next:
                            split_xsT(st, j + 1, 1 - st.parity)
                        if st.own:
                            finish_attention(st, j, 0, st.parity)
                    if i == 6:
                        if st.old:
                            if not st.own:
                                finish_layer1(st, j - 1, 1)
                            store_norm(j - 1, 0)
                        if st.own:
                            add_residual0(st, j, 0, st.parity)
                            statistics(y, mv, 0, j, half_stats1, stat1_ready)
                        if st.old and st.own:
                            take_u(j - 1, 1, True)
                    if i == 7:
                        if st.old and st.own:
                            finish_layer1(st, j - 1, 1)
                        if st.own:
                            take_h(j, 2)
                        if st.old:
                            store_norm(j - 1, 1)

            steps(dve, one_step)


_INS = ["x", "adj", "L0_gnn_W_a", "L0_gnn_bias", "L1_gnn_weight", "L1_gnn_bias"]
_OUTS = [((8, 1024, 128), "float32")]


def kernel(**inputs):
    import numpy as _np
    import concourse.bacc as _bacc
    from concourse import mybir as _mybir
    from concourse.bass_utils import run_bass_kernel_spmd as _run

    nc = _bacc.Bacc("TRN2", target_bir_lowering=False, num_devices=1)
    arrays, args = {}, []
    for name in _INS:
        a = _np.ascontiguousarray(inputs[name])
        arrays[f"in_{name}_dram"] = a
        args.append(nc.dram_tensor(f"in_{name}_dram", a.shape, _mybir.dt.from_np(a.dtype), kind="ExternalInput").ap())
    for i, (shape, dtype) in enumerate(_OUTS):
        dt = _mybir.dt.from_np(_np.dtype(dtype))
        args.append(nc.dram_tensor(f"out_{i}_dram", shape, dt, kind="ExternalOutput").ap())
    gnn_kernel(nc, *args)
    r = _run(nc, [arrays], core_ids=[0])
    return r.results[0]["out_0_dram"]
```
